# Optimizing a Trainium2 kernel written in Bass

```python
import numpy as np
import jax
import jax.numpy as jnp

def _softmax(x, axis=-1):
    return jax.nn.softmax(x, axis=axis)

def _gelu(x):
    return jax.nn.gelu(x, approximate=True)

def _silu(x):
    return jax.nn.silu(x)

def _sigmoid(x):
    return jax.nn.sigmoid(x)

def _layernorm(x, axis=-1, eps=1e-05):
    m = jnp.mean(x, axis=axis, keepdims=True)
    v = jnp.var(x, axis=axis, keepdims=True)
    return (x - m) / jnp.sqrt(v + eps)

def _scatter_add(tgt, idx, src, axis=0):
    return tgt.at[idx].add(src)

def _segment_sum(src, seg, n):
    return jax.ops.segment_sum(src, seg, n)
kernel_name = 'mk_adj_preln_d4_adj_r2_2b6bec'

def setup_inputs(seed: int=0):
    np.random.seed(seed)
    _w = jnp.asarray

    def _rec_inputs():
        import jax
        import jax.numpy as jnp
        _gk = jax.random.key(seed)
        x = -0.000929 + 1 * jax.random.normal(jax.random.fold_in(_gk, 1), (8192, 128), jnp.float32)
        _w = (1.0 + jnp.arange(8192, dtype=jnp.float32)) ** (-0.5)
        _w = _w / _w.mean()
        _pij = jnp.clip(0.000976562 * _w[:, None] * _w[None, :], 0.0, 1.0)
        _a = jax.random.uniform(jax.random.fold_in(_gk, 2), (8192, 8192)) < _pij
        adj = _a.astype(jnp.int32)
        return (x, adj)
    x, adj = _rec_inputs()

    def _L0_gnn_setup():
        import jax, jax.numpy as jnp
        import numpy as np
        ALPHA = 0.2
        NEG_BIG = -9000000000000000.0
        key = jax.random.key(seed)
        k1, k2, k3, k4 = jax.random.split(key, 4)
        N, F_IN, F_OUT = (4096, 128, 128)
        h = jax.random.normal(k1, (N, F_IN), dtype=jnp.float32)
        adj = jax.random.randint(k2, (N, N), 0, 2, dtype=jnp.int32)
        W = jax.random.normal(k3, (F_IN, F_OUT), dtype=jnp.float32) * (1.0 / np.sqrt(F_IN))
        a = jax.random.normal(k4, (2 * F_OUT, 1), dtype=jnp.float32) * (1.0 / np.sqrt(2 * F_OUT))
        return {'h': h, 'adj': adj, 'W': W, 'a': a}
    _L0_gnn_all = _L0_gnn_setup()
    _L0_gnn_in = {k: v for k, v in _L0_gnn_all.items() if k in ('W', 'a')}
    del _L0_gnn_all

    def _L1_gnn_setup():
        import jax, jax.numpy as jnp
        import numpy as np
        N = 4096
        D_IN = 128
        D_OUT = 128
        ALPHA = 0.2
        NEG = -9000000000000000.0
        key = jax.random.key(seed)
        k1, k2, k3, k4 = jax.random.split(key, 4)
        input = jax.random.normal(k1, (N, D_IN), dtype=jnp.float32)
        adj = jax.random.randint(k2, (N, N), 0, 2, dtype=jnp.int32)
        lim_w = 1.414 * np.sqrt(6.0 / (D_IN + D_OUT))
        W = jax.random.uniform(k3, (D_IN, D_OUT), jnp.float32, -lim_w, lim_w)
        lim_a = 1.414 * np.sqrt(6.0 / (2 * D_OUT + 1))
        a = jax.random.uniform(k4, (2 * D_OUT, 1), jnp.float32, -lim_a, lim_a)
        return {'input': input, 'adj': adj, 'W': W, 'a': a}
    _L1_gnn_all = _L1_gnn_setup()
    _L1_gnn_in = {k: v for k, v in _L1_gnn_all.items() if k in ('W', 'a')}
    del _L1_gnn_all

    def _L2_gnn_setup():
        import jax, jax.numpy as jnp
        import numpy as np
        N = 4096
        IN = 128
        OUT = 128
        THR = 0.0001
        ALPHA = 0.2
        NEG = -1000000000.0
        key = jax.random.key(seed)
        k1, k2, k3, k4 = jax.random.split(key, 4)
        inp = jax.random.normal(k1, (N, IN), jnp.float32)
        W = jax.random.normal(k2, (IN, OUT), jnp.float32) * (1.414 * np.sqrt(2.0 / (IN + OUT)))
        a = jax.random.normal(k3, (2 * OUT, 1), jnp.float32) * (1.414 * np.sqrt(2.0 / (2 * OUT + 1)))
        adj = jax.random.randint(k4, (N, N), 0, 2, jnp.int32)
        return {'input': inp, 'W': W, 'a': a, 'adj': adj, 'M': N}
    _L2_gnn_all = _L2_gnn_setup()
    _L2_gnn_in = {k: v for k, v in _L2_gnn_all.items() if k in ('W', 'a')}
    del _L2_gnn_all

    def _L3_gnn_setup():
        import jax, jax.numpy as jnp
        import numpy as np
        N = 4096
        IN_F = 128
        OUT_F = 128
        ALPHA = 0.2
        NEG_INF = -9000000000000000.0
        key = jax.random.key(seed)
        k1, k2, k3, k4 = jax.random.split(key, 4)
        h = jax.random.normal(k1, (N, IN_F), dtype=jnp.float32)
        adj = jax.random.randint(k2, (N, N), 0, 2, dtype=jnp.int32)
        W = jax.random.normal(k3, (IN_F, OUT_F), dtype=jnp.float32) * (1.0 / np.sqrt(IN_F))
        limit = 1.414 * np.sqrt(6.0 / (2 * OUT_F + 1))
        a = jax.random.uniform(k4, (2 * OUT_F, 1), dtype=jnp.float32, minval=-limit, maxval=limit)
        return {'h': h, 'adj': adj, 'W': W, 'a': a}
    _L3_gnn_all = _L3_gnn_setup()
    _L3_gnn_in = {k: v for k, v in _L3_gnn_all.items() if k in ('W', 'a')}
    del _L3_gnn_all
    return {'x': x, 'adj': adj, 'L0_gnn_W': _L0_gnn_in['W'], 'L0_gnn_a': _L0_gnn_in['a'], 'L1_gnn_W': _L1_gnn_in['W'], 'L1_gnn_a': _L1_gnn_in['a'], 'L2_gnn_W': _L2_gnn_in['W'], 'L2_gnn_a': _L2_gnn_in['a'], 'L3_gnn_W': _L3_gnn_in['W'], 'L3_gnn_a': _L3_gnn_in['a']}

def reference(x, adj, L0_gnn_W, L0_gnn_a, L1_gnn_W, L1_gnn_a, L2_gnn_W, L2_gnn_a, L3_gnn_W, L3_gnn_a):
    import jax
    import jax.numpy as jnp

    def _L0_gnn_ref(h, adj, W, a):
        import jax, jax.numpy as jnp
        import numpy as np
        ALPHA = 0.2
        NEG_BIG = -9000000000000000.0
        Wh = h @ W
        F_out = Wh.shape[1]
        a1 = a[:F_out, 0]
        a2 = a[F_out:, 0]
        e = (Wh @ a1)[:, None] + (Wh @ a2)[None, :]
        e = jnp.where(e >= 0, e, ALPHA * e)
        scores = jnp.where(adj > 0, e, NEG_BIG)
        attention = jax.nn.softmax(scores, axis=1)
        return attention @ Wh

    def _L1_gnn_ref(input, adj, W, a):
        import jax, jax.numpy as jnp
        import numpy as np
        N = 4096
        D_IN = 128
        D_OUT = 128
        ALPHA = 0.2
        NEG = -9000000000000000.0
        h = input @ W
        a1 = a[:D_OUT, 0]
        a2 = a[D_OUT:, 0]
        e = (h @ a1)[:, None] + (h @ a2)[None, :]
        e = jnp.where(e > 0, e, ALPHA * e)
        e = jnp.where(adj > 0, e, NEG)
        attention = jax.nn.softmax(e, axis=1)
        h_prime = attention @ h
        return jax.nn.elu(h_prime)

    def _L2_gnn_ref(input, W, a, adj, M):
        import jax, jax.numpy as jnp
        import numpy as np
        N = 4096
        IN = 128
        OUT = 128
        THR = 0.0001
        ALPHA = 0.2
        NEG = -1000000000.0
        h = input @ W
        a_src = a[:OUT, 0]
        a_dst = a[OUT:, 0]
        e = jax.nn.leaky_relu((h[:M] @ a_src)[:, None] + (h @ a_dst)[None, :], negative_slope=ALPHA)
        valid = (adj[:M] > 0) & (h.sum(axis=1) != 0)[None, :]
        att = jax.nn.softmax(jnp.where(valid, e, NEG), axis=1)
        att = jnp.where(valid, att, 0.0)
        L = valid.sum(axis=1).astype(h.dtype)
        top = att.max(axis=1)
        attention = jnp.where(att >= THR, att, 0.0) * L[:, None]
        attention = jnp.where((top > THR)[:, None], attention, 0.0)
        h_prime = attention @ h
        return jax.nn.elu(h[:M] + h_prime)

    def _L3_gnn_ref(h, adj, W, a):
        import jax, jax.numpy as jnp
        import numpy as np
        N = 4096
        IN_F = 128
        OUT_F = 128
        ALPHA = 0.2
        NEG_INF = -9000000000000000.0
        Wh = h @ W
        a1 = a[:OUT_F, 0]
        a2 = a[OUT_F:, 0]
        s1 = Wh @ a1
        s2 = Wh @ a2
        e = jax.nn.leaky_relu(s1[:, None] + s2[None, :], negative_slope=ALPHA)
        masked = jnp.where(adj > 0, e, NEG_INF)
        attention = jax.nn.softmax(masked, axis=1)
        h_prime = attention @ Wh
        return jax.nn.elu(h_prime)
    h = jnp.maximum(_layernorm(x, axis=-1), 0.0)
    x = x + _L0_gnn_ref(h, adj, L0_gnn_W, L0_gnn_a)
    h = jnp.maximum(_layernorm(x, axis=-1), 0.0)
    x = x + _L1_gnn_ref(h, adj, L1_gnn_W, L1_gnn_a)
    h = jnp.maximum(_layernorm(x, axis=-1), 0.0)
    x = x + _L2_gnn_ref(h, L2_gnn_W, L2_gnn_a, adj, 8192)
    h = jnp.maximum(_layernorm(x, axis=-1), 0.0)
    x = x + _L3_gnn_ref(h, adj, L3_gnn_W, L3_gnn_a)
    return x

_drawn_inputs = setup_inputs


def setup_inputs(seed=0):
    import zlib

    import numpy as np

    out = dict(_drawn_inputs(seed))
    spreads = {}
    factors = {'L3_gnn_a': 6.484}
    for name, (base, spread) in spreads.items():
        noise = np.random.default_rng([zlib.crc32(name.encode()), seed]).standard_normal(out[name].shape)
        drawn = base * np.exp(spread * noise) if base else spread * noise
        out[name] = jnp.asarray(drawn.astype(out[name].dtype))
    for name, factor in factors.items():
        out[name] = (out[name] * factor).astype(out[name].dtype)
    return out
```

```python
from contextlib import ExitStack

import numpy as np

import concourse.bass as bass
from concourse import mybir

P = 128
F = 128
N = 8192
BLOCKS = 4
W = P * BLOCKS
GROUPS = N // W
KT = N // P
CHUNKS = 4
JC = KT // CHUNKS
WORDS = W // 16
RING = 8
AJ = 4
PIECES = KT // AJ
ADJ_RING = 4
VRING = 2
ONE = 0x4000
MASK_VALUE = 2.0
ALPHA = 0.2
EPS = 1e-5
THR = 1e-4
BIG = 2.0 ** 60
LN_SHIFT = 43

F32 = mybir.dt.float32
BF16 = mybir.dt.bfloat16
U16 = mybir.dt.uint16
I32 = mybir.dt.int32
ALU = mybir.AluOpType
ACT = mybir.ActivationFunctionType
AX = mybir.AxisListType
RMAX = bass.bass_isa.ReduceOp.max

SWEEPS = [(0, "full"), (1, "full"), (2, "count"), (2, "kept"), (3, "full")]


class Group:

    def __init__(self, half, parity):
        self.half, self.parity = half, parity
        self.value = half * 2 + parity


def every_group(eng, body, tail):
    body(Group(0, 0), None, True)
    with eng.Fori(0, GROUPS // 2 - 1) as p:
        body(Group(p, 1), Group(p, 0), True)
        body(Group(p + 1, 0), Group(p, 1), True)
    body(Group(GROUPS // 2 - 1, 1), Group(GROUPS // 2 - 1, 0), False)
    tail(Group(GROUPS // 2 - 1, 1))


class Chain:

    def __init__(self, eng, sem):
        self.eng, self.sem, self.base, self.n = eng, sem, 0, 0

    def at(self, base):
        self.base, self.n = base, 0

    def __call__(self, ins):
        self.n += 1
        ins.then_inc(self.sem, 1)
        self.eng.wait_ge(self.sem, self.base + self.n)


def build(nc, x, adj, ws, avs, out):
    x_rows = x.rearrange("(g q p) f -> g p q f", q=BLOCKS, p=P)
    out_rows = out.rearrange("(g q p) f -> g p q f", q=BLOCKS, p=P)
    xs = nc.dram_tensor("x_between_layers", (N, F), F32).ap()
    xs_rows = xs.rearrange("(g q p) f -> g p q f", q=BLOCKS, p=P)
    adj_pieces = adj.rearrange("(g q p) (k c) -> g k p q c", q=BLOCKS, p=P, c=AJ * P)

    with ExitStack() as ctx:
        def sb(name, shape, dt):
            return ctx.enter_context(nc.sbuf_tensor(name, shape, dt))

        def ps(name, shape):
            return ctx.enter_context(nc.psum_tensor(name, shape, F32))

        def sem(name):
            return ctx.enter_context(nc.semaphore(name))

        bits = sb("bits", [P, GROUPS, KT, WORDS], U16)
        vals = sb("vals", [P, KT, F + 1], F32)
        wh = sb("wh", [P, KT, F], F32)
        mask = sb("mask", [P, 2, JC, W], U16)
        q = sb("q", [P, RING, W], F32)
        rrow = sb("rrow", [P, 2, W], F32)
        taurow = sb("taurow", [P, 2, W], F32)
        keep = sb("keep", [P, VRING, 2, W], BF16)
        diag = sb("diag", [P, BLOCKS, P], F32)
        xin = sb("xin", [P, BLOCKS, F], F32)
        xnew = sb("xnew", [P, BLOCKS, F], F32)
        e = sb("e", [P, BLOCKS, F], F32)
        hT = sb("hT", [P, BLOCKS, F], F32)
        w_sb = sb("w_sb", [P, 4, F], F32)
        a_sb = sb("a_sb", [P, 4, 2], F32)
        wa = sb("wa", [P, 4, 2], F32)
        ident = sb("ident", [P, P], F32)
        ones = sb("ones", [P, P], F32)
        nth = sb("nth", [P, P], F32)
        packer = sb("packer", [P, BLOCKS, WORDS], BF16)
        mean = sb("mean", [P, F], F32)
        s = sb("s", [P, 2, KT], F32)
        smax = sb("smax", [P, 1], F32)
        S = sb("S", [P, 1], F32)
        shift = sb("shift", [P, 2], F32)
        R = sb("R", [P, KT], F32)
        D = sb("D", [P, KT], F32)
        r = sb("r", [P, KT], F32)
        tau = sb("tau", [P, KT], F32)
        t1 = sb("t1", [P, KT], F32)
        t2 = sb("t2", [P, KT], F32)
        sbig = sb("sbig", [P, KT], F32)
        valid = sb("valid", [P, KT], F32)
        validb = sb("validb", [P, KT], BF16)
        den = sb("den", [P, KT], F32)
        cnt = sb("cnt", [P, KT], F32)
        kappa = sb("kappa", [P, KT], F32)
        den4 = sb("den4", [P, BLOCKS], F32)
        none4 = sb("none4", [P, BLOCKS], F32)
        rec4 = sb("rec4", [P, BLOCKS], F32)
        stats = sb("stats", [P, BLOCKS, 6], F32)
        mean2 = sb("mean2", [P, BLOCKS], F32)
        ve = sb("ve", [P, BLOCKS], F32)
        sd = sb("sd", [P, BLOCKS], F32)
        rs = sb("rs", [P, BLOCKS], F32)
        rt = sb("rt", [P, BLOCKS], F32)
        nm = sb("nm", [P, BLOCKS], F32)

        acc = [ps(f"acc{k}", [P, 2, 512]) for k in range(2)]
        ps_bc = ps("ps_bc", [P, 512])
        ps_tr = ps("ps_tr", [P, 512])
        ps_wh = ps("ps_wh", [P, 512])
        ps_s = ps("ps_s", [P, 512])

        o, h, wT = xnew, e, hT
        adj_int = mask[:, :, :, :].rearrange("p a b c -> p (a b c)").bitcast(I32).rearrange(
            "p (n q c) -> p n q c", n=ADJ_RING, q=BLOCKS)
        adj_bf = q[:, :, :].rearrange("p a b -> p (a b)").bitcast(BF16).rearrange(
            "p (n q c) -> p n q c", n=ADJ_RING, q=BLOCKS)
        mask_bf = mask[:, :, :, :].rearrange("p a b c -> p (a b c)").bitcast(BF16).rearrange(
            "p (a b c) -> p a b c", a=2, b=JC)
        pack_bank = [acc[k // 2][:, k % 2, :] for k in range(4)]

        consts_ready = sem("consts_ready")
        weights_in = sem("weights_in")
        wT_done = sem("wT_done")
        wT_copied = sem("wT_copied")
        wa_done = sem("wa_done")
        wa_copied = sem("wa_copied")
        adj_in = [sem(f"adj_in{k}") for k in range(ADJ_RING)]
        adj_binary = sem("adj_binary")
        adj_packed = sem("adj_packed")
        bits_ready = sem("bits_ready")
        mask_ready = sem("mask_ready")
        q_ready = sem("q_ready")
        q_used = sem("q_used")
        acc_free = sem("acc_free")
        diag_ready = sem("diag_ready")
        row_done = sem("row_done")
        row_ready = sem("row_ready")
        keep_ready = sem("keep_ready")
        keep_used = sem("keep_used")
        mask_kept = sem("mask_kept")
        var_ready = [sem(f"var_ready{k}") for k in range(4)]
        sd_ready = [sem(f"sd_ready{k}") for k in range(4)]
        norm_ready = [sem(f"norm_ready{k}") for k in range(4)]
        h_ready = [sem(f"h_ready{k}") for k in range(4)]
        tr_done = [sem(f"tr_done{k}") for k in range(4)]
        hT_ready = [sem(f"hT_ready{k}") for k in range(4)]
        wh_done = [sem(f"wh_done{k}") for k in range(4)]
        wh_ready = [sem(f"wh_ready{k}") for k in range(4)]
        ln_chain = [sem(f"ln_chain{k}") for k in range(4)]
        out_chain = [sem(f"out_chain{k}") for k in range(5)]
        elu_arg = [sem(f"elu_arg{k}") for k in range(4)]
        elu_exp = [sem(f"elu_exp{k}") for k in range(4)]
        x_new = [sem(f"x_new{k}") for k in range(4)]
        x_in = [[sem(f"x_in{k}_{b}") for b in range(2)] for k in range(5)]
        x_out = [[sem(f"x_out{k}_{b}") for b in range(2)] for k in range(4)]
        smax_ready = sem("smax_ready")
        S_ready = sem("S_ready")
        mean_done = sem("mean_done")
        shift_ready = sem("shift_ready")
        exps_ready = sem("exps_ready")
        vals_ready = sem("vals_ready")
        edge_chain = sem("edge_chain")
        log_arg = sem("log_arg")
        log_ready = sem("log_ready")

        rows_of = [1, 1, 1, 2, 1]
        rows_before = [sum(rows_of[:k]) * GROUPS for k in range(5)]

        mean_index = {0: 0, 1: 1, 3: 2}
        CONSTS = 5 + 16

        block = ctx.enter_context(nc.Block())

        @block.sync
        def _(sp):
            for k in range(4):
                sp.dma_start(w_sb[:, k, :], ws[k]).then_inc(weights_in, 16)
                for c in range(2):
                    sp.dma_start(a_sb[:, k, c:c + 1], avs[k][c * F:(c + 1) * F, :]).then_inc(weights_in, 16)

            def load_rows(k, src, g):
                sp.dma_start(xin[:, :, :], src[g.value]).then_inc(x_in[k][g.parity], 16)

            def pieces(g):
                for k in range(PIECES):
                    if k == 3:
                        sp.wait_ge(h_ready[0], g.value)
                        load_rows(4, x_rows, g)
                    slot = k % ADJ_RING
                    sp.wait_ge(adj_binary, g.value * PIECES + (k + 1 - ADJ_RING))
                    sp.dma_start(adj_int[:, slot, :, :], adj_pieces[g.value, k]).then_inc(adj_in[slot], 16)

            def pieces_first():
                g = Group(0, 0)
                load_rows(4, x_rows, g)
                for k in range(PIECES):
                    slot = k % ADJ_RING
                    if k >= ADJ_RING:
                        sp.wait_ge(adj_binary, k + 1 - ADJ_RING)
                    sp.dma_start(adj_int[:, slot, :, :], adj_pieces[0, k]).then_inc(adj_in[slot], 16)

            pieces_first()
            pieces(Group(0, 1))
            with sp.Fori(1, GROUPS // 2) as p:
                pieces(Group(p, 0))
                pieces(Group(p, 1))

            for k in range(4):
                src = x_rows if k == 0 else xs_rows
                dst = out_rows if k == 3 else xs_rows
                if k == 0:
                    sp.wait_ge(h_ready[0], GROUPS)
                load_rows(k, src, Group(0, 0))

                def store(g, load_next):
                    sp.wait_ge(x_new[k], g.value + 1)
                    sp.dma_start(dst[g.value], xnew[:, :, :]).then_inc(x_out[k][g.parity], 16)
                    if load_next:
                        sp.wait_ge(x_out[k][g.parity], g.half * 16 + 16)
                        load_rows(k, src, Group(g.half + g.parity, 1 - g.parity))

                with sp.Fori(0, GROUPS // 2 - 1) as p:
                    store(Group(p, 0), True)
                    store(Group(p, 1), True)
                store(Group(GROUPS // 2 - 1, 0), True)
                store(Group(GROUPS // 2 - 1, 1), False)
                for b in range(2):
                    sp.wait_ge(x_out[k][b], 16 * (GROUPS // 2))

        @block.gpsimd
        def _(pool):
            nc.gpsimd.memset(ident[:, :], 0.0).then_inc(consts_ready, 1)
            nc.gpsimd.memset(packer[:, :, :], 0.0).then_inc(consts_ready, 1)
            nc.gpsimd.memset(ones[:, :], 1.0).then_inc(consts_ready, 1)
            nc.gpsimd.memset(nth[:, :], 1.0 / N).then_inc(consts_ready, 1)
            pool.wait_ge(consts_ready, 4)
            nc.gpsimd.affine_select(out=ident[:, :], in_=ident[:, :], compare_op=ALU.not_equal, fill=1.0,
                                    base=0, pattern=[[-1, P]], channel_multiplier=1).then_inc(consts_ready, 1)
            step = 5
            for b in range(BLOCKS):
                for m in range(4):
                    nc.gpsimd.affine_select(out=packer[:, b, :], in_=packer[:, b, :], compare_op=ALU.not_equal,
                                            fill=float(2 ** (4 * b + m)), base=-WORDS * m,
                                            pattern=[[-1, WORDS]], channel_multiplier=1).then_inc(consts_ready, 1)
                    step += 1
                    pool.wait_ge(consts_ready, step)
            for k in range(4):
                pool.wait_ge(smax_ready, k + 1)
                nc.gpsimd.partition_all_reduce(S[:, :], smax[:, :], P, RMAX).then_inc(S_ready, 1)

        @block.vector
        def _(dve):
            edge = Chain(dve, edge_chain)
            LN_STEPS = 9

            def stats_of(k, xt, g):
                ln = Chain(dve, ln_chain[k])
                ln.at(g.value * LN_STEPS)
                for b in range(BLOCKS):
                    last = nc.vector.bn_stats(stats[:, b, :], xt[:, b, :])
                ln(last)
                nc.vector.tensor_tensor(mean2[:, :], stats[:, :, 1], stats[:, :, 4], ALU.add)
                nc.vector.tensor_tensor(ve[:, :], stats[:, :, 2], stats[:, :, 5], ALU.add)
                ln(nc.vector.tensor_tensor(rt[:, :], stats[:, :, 1], stats[:, :, 4], ALU.subtract))
                ln(nc.vector.tensor_tensor(rt[:, :], rt[:, :], rt[:, :], ALU.mult))
                ln(nc.vector.scalar_tensor_tensor(ve[:, :], rt[:, :], F / 4.0, ve[:, :], ALU.mult, ALU.add))
                nc.vector.tensor_scalar(ve[:, :], ve[:, :], 1.0 / F, EPS, ALU.mult, ALU.add)\
                    .then_inc(var_ready[k], 1)

            def scales_of(k, g):
                ln = Chain(dve, ln_chain[k])
                ln.at(g.value * LN_STEPS + 4)
                dve.wait_ge(sd_ready[k], g.value + 1)
                ln(nc.vector.reciprocal(rs[:, :], sd[:, :]))
                ln(nc.vector.tensor_tensor(rt[:, :], rs[:, :], rs[:, :], ALU.mult))
                ln(nc.vector.tensor_tensor(rt[:, :], rt[:, :], ve[:, :], ALU.mult))
                ln(nc.vector.tensor_scalar(rt[:, :], rt[:, :], -0.5, 1.5, ALU.mult, ALU.add))
                ln(nc.vector.tensor_tensor(rs[:, :], rs[:, :], rt[:, :], ALU.mult))
                assert ln.n == LN_STEPS - 4
                nc.vector.scalar_tensor_tensor(nm[:, :], mean2[:, :], -0.5, rs[:, :], ALU.mult, ALU.mult)\
                    .then_inc(norm_ready[k], 1)

            dve.wait_ge(consts_ready, CONSTS)

            def binary(g, first):
                for k in range(PIECES):
                    slot = k % ADJ_RING
                    dve.wait_ge(adj_in[slot], (g.value * (PIECES // ADJ_RING) + (k // ADJ_RING + 1)) * 16)
                    if not first or k >= ADJ_RING:
                        dve.wait_ge(adj_packed, g.value * PIECES + (k + 1 - ADJ_RING))
                    nc.vector.tensor_scalar(adj_bf[:, slot, :, :], adj_int[:, slot, :, :], 0, None, ALU.is_gt)\
                        .then_inc(adj_binary, 1)
                    if k == 4:
                        dve.wait_ge(x_in[4][g.parity], g.half * 16 + 16)
                        stats_of(0, xin[:, :, :], g)
                    if k == 8:
                        scales_of(0, g)

            binary(Group(0, 0), True)
            binary(Group(0, 1), False)
            with dve.Fori(1, GROUPS // 2) as p:
                binary(Group(p, 0), False)
                binary(Group(p, 1), False)
            dve.wait_ge(adj_packed, GROUPS * PIECES)

            def diagonal(sw, g, n):
                if n < rows_of[sw]:
                    col = [r, tau][n]
                    before = rows_of[sw] * g.value + (rows_before[sw] + n)
                    if not isinstance(before, int) or before > 0:
                        dve.wait_ge(row_done, before)
                    for b in range(BLOCKS):
                        last = nc.vector.tensor_scalar(diag[:, b, :], ident[:, :],
                                                       col[:, bass.ds(g.value * BLOCKS + b, 1)], None, ALU.mult)
                    last.then_inc(diag_ready, 1)

            def start_of_layer(k):
                dve.wait_ge(wh_ready[k], GROUPS)
                nc.vector.tensor_reduce(smax[:, :], s[:, 1, :], AX.X, ALU.max).then_inc(smax_ready, 1)
                if k == 2:
                    edge(nc.vector.tensor_reduce(t1[:, :], wh[:, :, :], AX.X, ALU.add))
                    edge(nc.vector.tensor_scalar(valid[:, :], t1[:, :], 0.0, None, ALU.not_equal))
                    edge(nc.vector.tensor_copy(validb[:, :], valid[:, :]))
                    nc.vector.tensor_scalar(sbig[:, :], s[:, 1, :], BIG, None, ALU.mult)
                dve.wait_ge(S_ready, k + 1)
                first = nc.vector.tensor_scalar(shift[:, 0:1], S[:, :], ALPHA - 1.0, None, ALU.mult)
                if k == 0:
                    first.then_inc(acc_free, 1)
                nc.vector.tensor_scalar(shift[:, 1:2], S[:, :], -ALPHA, None, ALU.mult)
                nc.vector.tensor_scalar(t2[:, :], s[:, 0, :], S[:, 0:1], 0.0, ALU.add, ALU.max)\
                    .then_inc(shift_ready, 1)
                dve.wait_ge(exps_ready, k + 1)
                if k == 2:
                    edge(nc.vector.tensor_tensor(D[:, :], D[:, :], valid[:, :], ALU.mult))
                diagonal([0, 1, 2, 4][k], Group(0, 0), 0)
                nc.vector.tensor_copy(vals[:, :, F], D[:, :])
                for c in range(CHUNKS):
                    t = slice(c * JC, (c + 1) * JC)
                    nc.vector.tensor_tensor(vals[:, t, 0:F], wh[:, t, :],
                                            D[:, t].rearrange("p (t o) -> p t o", o=1).broadcast_to([P, JC, F]),
                                            ALU.mult).then_inc(vals_ready, 1)
                if k != 2:
                    dve.wait_ge(mean_done, mean_index[k] + 1)
                    edge(nc.vector.tensor_copy(mean[:, :], ps_s[:, 128:128 + F]))

            def thresholds():
                edge(nc.vector.tensor_scalar(t1[:, :], den[:, :], THR / MASK_VALUE * 2.0 ** LN_SHIFT,
                                             2.0 ** -60, ALU.mult, ALU.max))
                nc.vector.tensor_scalar(t2[:, :], s[:, 0, :], S[:, 0:1], None, ALU.add).then_inc(log_arg, 1)
                dve.wait_ge(log_ready, 1)
                edge(nc.vector.scalar_tensor_tensor(t2[:, :], t2[:, :], ALPHA, t2[:, :], ALU.mult, ALU.max))
                edge(nc.vector.scalar_tensor_tensor(t1[:, :], t1[:, :], -LN_SHIFT * float(np.log(2.0)), t2[:, :],
                                                    ALU.add, ALU.add))
                edge(nc.vector.scalar_tensor_tensor(t1[:, :], t1[:, :], 1.0 / ALPHA, t1[:, :], ALU.mult, ALU.min))
                edge(nc.vector.tensor_tensor(tau[:, :], t1[:, :], s[:, 0, :], ALU.subtract))
                edge(nc.vector.tensor_scalar(t1[:, :], den[:, :], 0.0, None, ALU.is_equal))
                edge(nc.vector.tensor_tensor(t1[:, :], t1[:, :], den[:, :], ALU.add))
                edge(nc.vector.reciprocal(t1[:, :], t1[:, :]))
                edge(nc.vector.scalar_tensor_tensor(kappa[:, :], cnt[:, :], 1.0 / MASK_VALUE, t1[:, :],
                                                    ALU.mult, ALU.mult))

            def column(t, i):
                return t[:, i:i + 1]

            def chunk(sw, g, c):
                kind = SWEEPS[sw][1]
                done = (g.value + sw * GROUPS) * KT + c * JC
                buf = c % 2
                if kind == "count":
                    if not isinstance(done, int) or done >= 2 * JC:
                        dve.wait_ge(q_used, done - JC)
                for b in range(16):
                    op, amount = (ALU.logical_shift_left, 14 - b) if b <= 14 else (ALU.logical_shift_right, 1)
                    last = nc.vector.tensor_scalar(
                        mask[:, buf, :, b * WORDS:(b + 1) * WORDS],
                        bits[:, g.value, c * JC:(c + 1) * JC, :], amount, ONE, op, ALU.bitwise_and)
                last.then_inc(mask_ready, 1)
                dve.wait_ge(mask_ready, (g.value + sw * GROUPS) * CHUNKS + (c + 1))
                for j in range(JC):
                    if kind == "kept" and j % 2 == 0:
                        t = g.value * (KT // 2) + (c * JC + j) // 2
                        dve.wait_ge(keep_ready, t + 1)
                        pair = mask_bf[:, buf, j:j + 2, :]
                        nc.vector.tensor_tensor(pair, pair, keep[:, ((c * JC + j) // 2) % VRING, :, :], ALU.min)\
                            .then_inc(mask_kept, 1)
                        dve.wait_ge(mask_kept, t + 1)
                    tile = done + j
                    if not isinstance(tile, int) or tile >= RING:
                        dve.wait_ge(q_used, tile + (1 - RING))
                    nc.vector.scalar_tensor_tensor(
                        q[:, j % RING, :], rrow[:, g.parity, :], column(R, c * JC + j), mask_bf[:, buf, j, :],
                        ALU.max, ALU.mult).then_inc(q_ready, 1)

            OUT_STEPS = {"full": 5, "count": 1, "kept": 2}

            def outputs(sw, g):
                k, kind = SWEEPS[sw]
                a = acc[g.parity]
                chain = Chain(dve, out_chain[sw])
                chain.at(g.value * OUT_STEPS[kind])
                dve.wait_ge(q_used, (g.value + (sw * GROUPS + 1)) * KT)
                cols = bass.ds(g.value * BLOCKS, BLOCKS)
                if kind == "count":
                    chain(nc.vector.tensor_copy(den[:, cols], a[:, 0, 0:BLOCKS]))
                    nc.vector.tensor_copy(cnt[:, cols], a[:, 0, BLOCKS:2 * BLOCKS]).then_inc(acc_free, 1)
                    dve.wait_ge(acc_free, g.value + (sw * GROUPS + 2))
                    return
                dve.wait_ge(x_in[k][g.parity], g.half * 16 + 16)
                num = a[:, :, 0:2 * (F + 1)].rearrange("p a (b f) -> p a b f", b=2)[:, :, :, 0:F]
                o4 = o[:, :, :].rearrange("p (a b) f -> p a b f", a=2)
                if kind == "full":
                    dens = a[:, :, F:2 * (F + 1):F + 1]
                    d22 = den4[:, :].rearrange("p (a b) -> p a b", a=2)
                    chain(nc.vector.tensor_copy(d22, dens))
                    chain(nc.vector.tensor_scalar(none4[:, :], den4[:, :], 0.0, None, ALU.is_equal))
                    chain(nc.vector.tensor_tensor(den4[:, :], den4[:, :], none4[:, :], ALU.add))
                    chain(nc.vector.reciprocal(rec4[:, :], den4[:, :]))
                    scale = rec4[:, :]
                else:
                    chain(nc.vector.tensor_copy(rec4[:, :], kappa[:, cols]))
                    scale = rec4[:, :]
                scale = scale.rearrange("p (a b o) -> p a b o", a=2, o=1).broadcast_to([P, 2, 2, F])
                ins = nc.vector.tensor_tensor(o4, num, scale, ALU.mult)
                ins.then_inc(acc_free, 1)
                dve.wait_ge(acc_free, g.value + (sw * GROUPS + 2))
                if kind == "full":
                    for b in range(BLOCKS):
                        last = nc.vector.scalar_tensor_tensor(o[:, b, :], mean[:, :], none4[:, b:b + 1], o[:, b, :],
                                                              ALU.mult, ALU.add)
                    chain(last)
                else:
                    chain(nc.vector.tensor_tensor(o[:, :, :], o[:, :, :], wh[:, cols, :], ALU.add))
                if k == 0:
                    nc.vector.tensor_tensor(xnew[:, :, :], xin[:, :, :], o[:, :, :], ALU.add)\
                        .then_inc(x_new[k], 1)
                else:
                    nc.vector.tensor_scalar(e[:, :, :], o[:, :, :], 0.0, None, ALU.min).then_inc(elu_arg[k], 1)

            def new_rows(sw, g):
                k, kind = SWEEPS[sw]
                if kind == "count":
                    return
                xn = xnew[:, :, :]
                if k > 0:
                    nc.vector.scalar_tensor_tensor(o[:, :, :], o[:, :, :], 0.0, xin[:, :, :],
                                                   ALU.max, ALU.add).then_inc(elu_arg[k], 1)
                    dve.wait_ge(elu_arg[k], g.value * 2 + 2)
                    dve.wait_ge(elu_exp[k], g.value + 1)
                    nc.vector.scalar_tensor_tensor(xn, e[:, :, :], -1.0, o[:, :, :], ALU.add, ALU.add)\
                        .then_inc(x_new[k], 1)
                dve.wait_ge(x_new[k], g.value + 1)
                if k < 3:
                    stats_of(k + 1, xn, g)

            def rows_scaled(sw, g):
                k, kind = SWEEPS[sw]
                if kind != "count" and k < 3:
                    scales_of(k + 1, g)

            def body(sw):
                def group(g, before, more):
                    n = rows_of[sw] * g.value + (rows_before[sw] + rows_of[sw])
                    dve.wait_ge(row_ready, n)
                    for c in range(CHUNKS):
                        chunk(sw, g, c)
                        if c == 0:
                            if before:
                                outputs(sw, before)
                            if more:
                                diagonal(sw, Group(g.half + g.parity, 1 - g.parity), 0)
                        if before and c == 1:
                            new_rows(sw, before)
                        if before and c == 2:
                            rows_scaled(sw, before)
                        if more and c == 2:
                            diagonal(sw, Group(g.half + g.parity, 1 - g.parity), 1)
                return group

            def last_tail(sw):
                def tail(g):
                    outputs(sw, g)
                    new_rows(sw, g)
                    rows_scaled(sw, g)
                return tail

            for sw, (k, kind) in enumerate(SWEEPS):
                if kind == "kept":
                    thresholds()
                    diagonal(sw, Group(0, 0), 0)
                    diagonal(sw, Group(0, 0), 1)
                else:
                    start_of_layer(k)
                every_group(dve, body(sw), last_tail(sw))

        @block.tensor
        def _(pe):
            def transposes(k, g):
                pe.wait_ge(h_ready[k], g.value + 1)
                for b in range(BLOCKS):
                    last = nc.tensor.transpose(ps_tr[:, b * P:(b + 1) * P], h[:, b, :], ident[:, :])
                last.then_inc(tr_done[k], 1)

            def project(k, g):
                pe.wait_ge(hT_ready[k], g.value + 1)
                for b in range(BLOCKS):
                    nc.tensor.matmul(ps_wh[:, b * F:(b + 1) * F], hT[:, b, :], w_sb[:, k, :], start=True, stop=True)
                for b in range(BLOCKS):
                    last = nc.tensor.matmul(ps_s[:, 2 * b:2 * b + 2], hT[:, b, :], wa[:, k, :],
                                            start=True, stop=True)
                last.then_inc(wh_done[k], 1)

            pe.wait_ge(weights_in, 16 * 12)
            pe.wait_ge(consts_ready, CONSTS)
            for k in range(4):
                last = nc.tensor.transpose(ps_tr[:, k * P:(k + 1) * P], w_sb[:, k, :], ident[:, :])
            last.then_inc(wT_done, 1)
            pe.wait_ge(wT_copied, 1)
            for k in range(4):
                last = nc.tensor.matmul(ps_s[:, 2 * k:2 * k + 2], wT[:, k, :], a_sb[:, k, :], start=True, stop=True)
            last.then_inc(wa_done, 1)
            pe.wait_ge(wa_copied, 1)

            def pack(g, first):
                for k in range(PIECES):
                    quarter, slot = k // 4, k % ADJ_RING
                    if not first and k % 4 == 0:
                        pe.wait_ge(bits_ready, g.value * 4 + (quarter - 3))
                    pe.wait_ge(adj_binary, g.value * PIECES + (k + 1))
                    for t in range(AJ):
                        at = ((k % 4) * AJ + t) * WORDS
                        for b in range(BLOCKS):
                            last = nc.tensor.matmul(pack_bank[quarter][:, at:at + WORDS],
                                                    adj_bf[:, slot, b, t * P:(t + 1) * P], packer[:, b, :],
                                                    start=(b == 0), stop=(b == BLOCKS - 1))
                    last.then_inc(adj_packed, 1)
                    if k == 12:
                        transposes(0, g)
                    if k == 14:
                        project(0, g)

            pack(Group(0, 0), True)
            pack(Group(0, 1), False)
            with pe.Fori(1, GROUPS // 2) as p:
                pack(Group(p, 0), False)
                pack(Group(p, 1), False)

            def spread(sw, g, n):
                if n < rows_of[sw]:
                    done = rows_of[sw] * g.value + (rows_before[sw] + n)
                    pe.wait_ge(diag_ready, done + 1)
                    if not isinstance(done, int) or done > 0:
                        pe.wait_ge(row_ready, done)
                    for b in range(BLOCKS):
                        last = nc.tensor.matmul(ps_bc[:, b * P:(b + 1) * P], ones[:, :], diag[:, b, :],
                                                start=True, stop=True)
                    last.then_inc(row_done, 1)

            def mean_row(k):
                pe.wait_ge(wh_ready[k], GROUPS)
                for t in range(KT):
                    last = nc.tensor.matmul(ps_s[:, 128:128 + F], nth[:, :], wh[:, t, :],
                                            start=(t == 0), stop=(t == KT - 1))
                last.then_inc(mean_done, 1)

            def sweep_chunk(sw, g, c, middle):
                kind = SWEEPS[sw][1]
                a = acc[g.parity]
                for j in range(JC):
                    t = c * JC + j
                    pe.wait_ge(q_ready, (g.value + sw * GROUPS) * KT + (t + 1))
                    for b in range(BLOCKS):
                        weights = q[:, j % RING, b * P:(b + 1) * P]
                        if kind == "count":
                            nc.tensor.matmul(a[:, 0, b:b + 1], weights, vals[:, t, F:F + 1],
                                             start=(t == 0 and b == 0), stop=(t == KT - 1),
                                             skip_group_check=True)
                            last = nc.tensor.matmul(a[:, 0, BLOCKS + b:BLOCKS + b + 1],
                                                    mask_bf[:, c % 2, j, b * P:(b + 1) * P], validb[:, t:t + 1],
                                                    start=False, stop=(t == KT - 1), skip_group_check=True)
                        else:
                            at = (b % 2) * (F + 1)
                            last = nc.tensor.matmul(a[:, b // 2, at:at + F + 1], weights, vals[:, t, :],
                                                    start=(t == 0 and b % 2 == 0), stop=(t == KT - 1),
                                                    skip_group_check=True)
                    last.then_inc(q_used, 1)
                    if j == JC // 2 - 1:
                        middle()

            def body(sw):
                k, kind = SWEEPS[sw]
                projects = kind != "count" and k < 3

                def group(g, before, more):
                    if not isinstance(g.value, int) or g.value + sw > 0:
                        pe.wait_ge(acc_free, g.value + sw * GROUPS)
                    for c in range(CHUNKS):
                        def middle():
                            if c == 3 and more:
                                spread(sw, Group(g.half + g.parity, 1 - g.parity), 1)
                            if c == 3 and before and projects:
                                transposes(k + 1, before)
                        sweep_chunk(sw, g, c, middle)
                        if c == 1 and more:
                            spread(sw, Group(g.half + g.parity, 1 - g.parity), 0)
                        if c == 3 and before and projects:
                            project(k + 1, before)
                return group

            def last_tail(sw):
                k, kind = SWEEPS[sw]

                def tail(g):
                    if kind != "count" and k < 3:
                        transposes(k + 1, g)
                        project(k + 1, g)
                return tail

            for sw, (k, kind) in enumerate(SWEEPS):
                spread(sw, Group(0, 0), 0)
                spread(sw, Group(0, 0), 1)
                if kind != "kept":
                    if k != 2:
                        mean_row(k)
                    pe.wait_ge(vals_ready, CHUNKS * (k + 1))
                every_group(pe, body(sw), last_tail(sw))

        @block.scalar
        def _(act):
            act.wait_ge(wT_done, 1)
            nc.scalar.activation(wT[:, :, :], ps_tr[:, :].rearrange("p (k f) -> p k f", k=4), ACT.Copy)\
                .then_inc(wT_copied, 1)
            act.wait_ge(wa_done, 1)
            nc.scalar.activation(wa[:, :, :], ps_s[:, 0:8].rearrange("p (k c) -> p k c", k=4), ACT.Copy)\
                .then_inc(wa_copied, 1)

            def deviations(k, g):
                act.wait_ge(var_ready[k], g.value + 1)
                nc.scalar.activation(sd[:, :], ve[:, :], ACT.Sqrt).then_inc(sd_ready[k], 1)

            def normalised(k, xt, g):
                act.wait_ge(norm_ready[k], g.value + 1)
                for b in range(BLOCKS):
                    last = nc.scalar.activation(h[:, b, :], xt[:, b, :], ACT.Relu, bias=nm[:, b:b + 1],
                                                scale=rs[:, b:b + 1])
                last.then_inc(h_ready[k], 1)

            def copy_hT(k, g):
                act.wait_ge(tr_done[k], g.value + 1)
                nc.scalar.activation(hT[:, :, :], ps_tr[:, :].rearrange("p (b f) -> p b f", b=BLOCKS), ACT.Copy)\
                    .then_inc(hT_ready[k], 1)

            def copy_wh(k, g):
                act.wait_ge(wh_done[k], g.value + 1)
                cols = bass.ds(g.value * BLOCKS, BLOCKS)
                nc.scalar.activation(wh[:, cols, :], ps_wh[:, :].rearrange("p (b f) -> p b f", b=BLOCKS), ACT.Copy)
                nc.scalar.activation(s[:, :, cols], ps_s[:, 0:2 * BLOCKS].rearrange("p (b c) -> p c b", c=2),
                                     ACT.Copy).then_inc(wh_ready[k], 1)

            def words(g):
                for quarter in range(4):
                    act.wait_ge(adj_packed, g.value * PIECES + 4 * (quarter + 1))
                    nc.scalar.activation(
                        bits[:, g.value, quarter * JC:(quarter + 1) * JC, :],
                        pack_bank[quarter].rearrange("p (t n) -> p t n", t=JC), ACT.Copy).then_inc(bits_ready, 1)
                    if quarter == 1:
                        deviations(0, g)
                        normalised(0, xin[:, :, :], g)
                    if quarter == 2:
                        copy_hT(0, g)
                copy_wh(0, g)

            with act.Fori(0, GROUPS // 2) as p:
                words(Group(p, 0))
                words(Group(p, 1))

            def copy_rows(sw, g, n):
                if n < rows_of[sw]:
                    row = [rrow, taurow][n]
                    act.wait_ge(row_done, rows_of[sw] * g.value + (rows_before[sw] + n + 1))
                    nc.scalar.activation(row[:, g.parity, :], ps_bc[:, :], ACT.Copy).then_inc(row_ready, 1)

            def elu_exp_of(k, g):
                act.wait_ge(elu_arg[k], g.value * 2 + 1)
                nc.scalar.activation(e[:, :, :], e[:, :, :], ACT.Exp).then_inc(elu_exp[k], 1)

            def keep_tile(g, t):
                n = g.value * (KT // 2) + t
                if not isinstance(n, int) or n >= VRING:
                    act.wait_ge(mask_kept, n + (1 - VRING))
                for j in range(2):
                    last = nc.scalar.activation(keep[:, t % VRING, j, :], taurow[:, g.parity, :], ACT.Relu,
                                                scale=-BIG, bias=sbig[:, 2 * t + j:2 * t + j + 1])
                last.then_inc(keep_ready, 1)

            def steps(sw, g, before, more):
                k, kind = SWEEPS[sw]
                todo = []
                if before and kind != "count" and k > 0:
                    todo.append((JC + 4, lambda: elu_exp_of(k, before)))
                if more:
                    todo.append((2 * JC + 4, lambda: copy_rows(sw, Group(g.half + g.parity, 1 - g.parity), 0)))
                if before and kind != "count" and k < 3:
                    xt = xnew[:, :, :]
                    todo.append((2 * JC + 8, lambda: deviations(k + 1, before)))
                    todo.append((3 * JC + 4, lambda: normalised(k + 1, xt, before)))
                if more:
                    todo.append((3 * JC + 12, lambda: copy_rows(sw, Group(g.half + g.parity, 1 - g.parity), 1)))
                if before and kind != "count" and k < 3:
                    todo.append((KT, lambda: copy_hT(k + 1, before)))
                    todo.append((KT, lambda: copy_wh(k + 1, before)))
                return todo

            def body(sw):
                kind = SWEEPS[sw][1]

                def group(g, before, more):
                    todo = steps(sw, g, before, more)
                    if kind == "kept":
                        act.wait_ge(row_ready, rows_of[sw] * g.value + (rows_before[sw] + 2))
                        for t in range(KT // 2):
                            while todo and todo[0][0] <= 2 * t:
                                todo.pop(0)[1]()
                            keep_tile(g, t)
                    for _, do in todo:
                        do()
                return group

            def last_tail(sw):
                k, kind = SWEEPS[sw]

                def tail(g):
                    if kind == "count":
                        return
                    if k > 0:
                        elu_exp_of(k, g)
                    if k < 3:
                        deviations(k + 1, g)
                        normalised(k + 1, xnew[:, :, :], g)
                        copy_hT(k + 1, g)
                        copy_wh(k + 1, g)
                return tail

            for sw, (k, kind) in enumerate(SWEEPS):
                if kind == "kept":
                    act.wait_ge(log_arg, 1)
                    nc.scalar.activation(t1[:, :], t1[:, :], ACT.Ln).then_inc(log_ready, 1)
                else:
                    act.wait_ge(shift_ready, k + 1)
                    nc.scalar.activation(R[:, :], s[:, 1, :], ACT.Exp, scale=1.0 - ALPHA, bias=shift[:, 0:1])
                    nc.scalar.activation(D[:, :], s[:, 1, :], ACT.Exp, scale=ALPHA, bias=shift[:, 1:2])
                    nc.scalar.activation(r[:, :], t2[:, :], ACT.Exp, scale=ALPHA - 1.0).then_inc(exps_ready, 1)
                copy_rows(sw, Group(0, 0), 0)
                copy_rows(sw, Group(0, 0), 1)
                every_group(act, body(sw), last_tail(sw))


_WS = [f"L{k}_gnn_W" for k in range(4)]
_AS = [f"L{k}_gnn_a" for k in range(4)]


def kernel(**inputs):
    import numpy as _np
    import concourse.bacc as _bacc
    from concourse import mybir as _mybir
    from concourse.bass_utils import run_bass_kernel_spmd as _run

    nc = _bacc.Bacc("TRN2", target_bir_lowering=False, num_devices=1)
    arrays, aps = {}, {}
    for name in ["x", "adj"] + _WS + _AS:
        a = _np.ascontiguousarray(inputs[name])
        arrays[f"in_{name}_dram"] = a
        aps[name] = nc.dram_tensor(f"in_{name}_dram", a.shape, _mybir.dt.from_np(a.dtype), kind="ExternalInput").ap()
    out = nc.dram_tensor("out_0_dram", (N, F), F32, kind="ExternalOutput").ap()
    build(nc, aps["x"], aps["adj"], [aps[n] for n in _WS], [aps[n] for n in _AS], out)
    r = _run(nc, [arrays], core_ids=[0])
    return r.results[0]["out_0_dram"]
```

```python
from contextlib import ExitStack

import numpy as np

import concourse.bass as bass
from concourse import mybir

P = 128
F = 128
N = 8192
BLOCKS = 4
W = P * BLOCKS
GROUPS = N // W
KT = N // P
CHUNKS = 4
JC = KT // CHUNKS
WORDS = W // 16
RING = 8
AJ = 4
PIECES = KT // AJ
ADJ_RING = 4
VRING = 2
ONE = 0x4000
MASK_VALUE = 2.0
ALPHA = 0.2
EPS = 1e-5
THR = 1e-4
BIG = 2.0 ** 60
LN_SHIFT = 43

F32 = mybir.dt.float32
BF16 = mybir.dt.bfloat16
U16 = mybir.dt.uint16
I32 = mybir.dt.int32
ALU = mybir.AluOpType
ACT = mybir.ActivationFunctionType
AX = mybir.AxisListType
RMAX = bass.bass_isa.ReduceOp.max

SWEEPS = [(0, "full"), (1, "full"), (2, "counted"), (3, "full"), (2, "kept")]
REDO = 4
MAIN = range(4)
REPROJECT = 4


def next_projection(sw):
    return REPROJECT if sw == REDO else sw + 1


def layer_of(projection):
    return min(projection, 3)


class Group:

    def __init__(self, half, parity):
        self.half, self.parity = half, parity
        self.value = half * 2 + parity


def every_group(eng, body, tail):
    body(Group(0, 0), None, True)
    with eng.Fori(0, GROUPS // 2 - 1) as p:
        body(Group(p, 1), Group(p, 0), True)
        body(Group(p + 1, 0), Group(p, 1), True)
    body(Group(GROUPS // 2 - 1, 1), Group(GROUPS // 2 - 1, 0), False)
    tail(Group(GROUPS // 2 - 1, 1))


class RedoGroup:

    def __init__(self, value):
        self.value = self.half = value
        self.parity = 0


class Chain:

    def __init__(self, eng, sem):
        self.eng, self.sem, self.base, self.n = eng, sem, 0, 0

    def at(self, base):
        self.base, self.n = base, 0

    def __call__(self, ins):
        self.n += 1
        ins.then_inc(self.sem, 1)
        self.eng.wait_ge(self.sem, self.base + self.n)


def build(nc, x, adj, ws, avs, out):
    x_rows = x.rearrange("(g q p) f -> g p q f", q=BLOCKS, p=P)
    out_rows = out.rearrange("(g q p) f -> g p q f", q=BLOCKS, p=P)
    xs = nc.dram_tensor("x_between_layers", (N, F), F32).ap()
    xs_rows = xs.rearrange("(g q p) f -> g p q f", q=BLOCKS, p=P)
    x3 = nc.dram_tensor("x_of_layer_3", (N, F), F32).ap()
    x3_rows = x3.rearrange("(g q p) f -> g p q f", q=BLOCKS, p=P)
    wh2 = nc.dram_tensor("wh_of_layer_2", (N, F), F32).ap()
    wh2_rows = wh2.rearrange("(g q p) f -> g p q f", q=BLOCKS, p=P)
    adj_pieces = adj.rearrange("(g q p) (k c) -> g k p q c", q=BLOCKS, p=P, c=AJ * P)

    with ExitStack() as ctx:
        def sb(name, shape, dt):
            return ctx.enter_context(nc.sbuf_tensor(name, shape, dt))

        def ps(name, shape):
            return ctx.enter_context(nc.psum_tensor(name, shape, F32))

        def sem(name):
            return ctx.enter_context(nc.semaphore(name))

        bits = sb("bits", [P, GROUPS, KT, WORDS], U16)
        vals = sb("vals", [P, KT, F + 1], F32)
        wh = sb("wh", [P, KT, F], F32)
        mask = sb("mask", [P, 2, JC, W], U16)
        q = sb("q", [P, RING, W], F32)
        rrow = sb("rrow", [P, 2, W], F32)
        taurow = sb("taurow", [P, W], F32)
        keep = sb("keep", [P, VRING, 2, W], BF16)
        diag = sb("diag", [P, BLOCKS, P], F32)
        xin = sb("xin", [P, BLOCKS, F], F32)
        xnew = sb("xnew", [P, BLOCKS, F], F32)
        e = sb("e", [P, BLOCKS, F], F32)
        hT = sb("hT", [P, BLOCKS, F], F32)
        w_sb = sb("w_sb", [P, 4, F], F32)
        a_sb = sb("a_sb", [P, 4, 2], F32)
        wa = sb("wa", [P, 4, 2], F32)
        ident = sb("ident", [P, P], F32)
        ones = sb("ones", [P, P], F32)
        nth = sb("nth", [P, P], F32)
        packer = sb("packer", [P, BLOCKS, WORDS], BF16)
        mean = sb("mean", [P, F], F32)
        s = sb("s", [P, 2, KT], F32)
        smax = sb("smax", [P, 1], F32)
        S = sb("S", [P, 1], F32)
        shift = sb("shift", [P, 2], F32)
        R = sb("R", [P, KT], F32)
        D = sb("D", [P, KT], F32)
        r = sb("r", [P, KT], F32)
        tau = sb("tau", [P, KT], F32)
        t1 = sb("t1", [P, KT], F32)
        t2 = sb("t2", [P, KT], F32)
        sbig = sb("sbig", [P, KT], F32)
        valid = sb("valid", [P, KT], F32)
        validb = sb("validb", [P, KT], BF16)
        den = sb("den", [P, KT], F32)
        s1_of_2 = sb("s1_of_2", [P, KT], F32)
        number = sb("number", [P, KT], F32)
        least = sb("least", [P, 2], F32)
        found = sb("found", [P, 2], F32)
        redo_groups = sb("redo_groups", [P, 1], I32)
        kappa = sb("kappa", [P, KT], F32)
        den4 = sb("den4", [P, BLOCKS], F32)
        none4 = sb("none4", [P, BLOCKS], F32)
        rec4 = sb("rec4", [P, BLOCKS], F32)
        stats = sb("stats", [P, BLOCKS, 6], F32)
        mean2 = sb("mean2", [P, BLOCKS], F32)
        ve = sb("ve", [P, BLOCKS], F32)
        sd = sb("sd", [P, BLOCKS], F32)
        rs = sb("rs", [P, BLOCKS], F32)
        rt = sb("rt", [P, BLOCKS], F32)
        nm = sb("nm", [P, BLOCKS], F32)

        acc = [ps(f"acc{k}", [P, 2, 512]) for k in range(2)]
        ps_bc = ps("ps_bc", [P, 512])
        ps_tr = ps("ps_tr", [P, 512])
        ps_wh = ps("ps_wh", [P, 512])
        ps_s = ps("ps_s", [P, 512])

        o, h, wT = xnew, e, hT
        wh_rows = diag
        adj_int = mask[:, :, :, :].rearrange("p a b c -> p (a b c)").bitcast(I32).rearrange(
            "p (n q c) -> p n q c", n=ADJ_RING, q=BLOCKS)
        adj_bf = q[:, :, :].rearrange("p a b -> p (a b)").bitcast(BF16).rearrange(
            "p (n q c) -> p n q c", n=ADJ_RING, q=BLOCKS)
        mask_bf = mask[:, :, :, :].rearrange("p a b c -> p (a b c)").bitcast(BF16).rearrange(
            "p (a b c) -> p a b c", a=2, b=JC)
        pack_bank = [acc[k // 2][:, k % 2, :] for k in range(4)]

        consts_ready = sem("consts_ready")
        weights_in = sem("weights_in")
        wT_done = sem("wT_done")
        wT_copied = sem("wT_copied")
        wa_done = sem("wa_done")
        wa_copied = sem("wa_copied")
        adj_in = [sem(f"adj_in{k}") for k in range(ADJ_RING)]
        adj_binary = sem("adj_binary")
        adj_packed = sem("adj_packed")
        bits_ready = sem("bits_ready")
        mask_ready = [sem("mask_ready"), sem("redo_mask_ready")]
        q_ready = [sem("q_ready"), sem("redo_q_ready")]
        q_used = [sem("q_used"), sem("redo_q_used")]
        acc_free = [sem("acc_free"), sem("redo_acc_free")]
        diag_ready = [sem("diag_ready"), sem("redo_diag_ready")]
        row_done = [sem("row_done"), sem("redo_row_done")]
        row_ready = [sem("row_ready"), sem("redo_row_ready")]
        keep_ready = sem("keep_ready")
        mask_kept = sem("mask_kept")
        var_ready = [sem(f"var_ready{k}") for k in range(5)]
        sd_ready = [sem(f"sd_ready{k}") for k in range(5)]
        norm_ready = [sem(f"norm_ready{k}") for k in range(5)]
        h_ready = [sem(f"h_ready{k}") for k in range(5)]
        tr_done = [sem(f"tr_done{k}") for k in range(5)]
        hT_ready = [sem(f"hT_ready{k}") for k in range(5)]
        wh_done = [sem(f"wh_done{k}") for k in range(5)]
        wh_ready = [sem(f"wh_ready{k}") for k in range(5)]
        ln_chain = [sem(f"ln_chain{k}") for k in range(5)]
        out_chain = [sem(f"out_chain{k}") for k in range(5)]
        elu_arg = [sem(f"elu_arg{k}") for k in range(5)]
        elu_exp = [sem(f"elu_exp{k}") for k in range(5)]
        x_new = [sem(f"x_new{k}") for k in range(5)]
        x_in = [[sem(f"x_in{k}_{b}") for b in range(2)] for k in range(6)]
        x_out = [[sem(f"x_out{k}_{b}") for b in range(2)] for k in range(4)]
        smax_ready = sem("smax_ready")
        S_ready = sem("S_ready")
        mean_done = sem("mean_done")
        shift_ready = sem("shift_ready")
        exps_ready = sem("exps_ready")
        vals_ready = sem("vals_ready")
        edge_chain = sem("edge_chain")
        log_arg = sem("log_arg")
        log_ready = sem("log_ready")
        redo_stored = sem("redo_stored")
        wh_rows_in = sem("wh_rows_in")
        redo_known = sem("redo_known")

        own = [0, 0, 0, 0, 1]
        groups_before = [k * GROUPS for k in MAIN] + [0]
        rows_of = [1, 1, 1, 1, 2]

        mean_index = {0: 0, 1: 1, 3: 2}
        CONSTS = 5 + 16

        block = ctx.enter_context(nc.Block())

        @block.sync
        def _(sp):
            for k in range(4):
                sp.dma_start(w_sb[:, k, :], ws[k]).then_inc(weights_in, 16)
                for c in range(2):
                    sp.dma_start(a_sb[:, k, c:c + 1], avs[k][c * F:(c + 1) * F, :]).then_inc(weights_in, 16)

            def load_rows(k, src, g):
                sp.dma_start(xin[:, :, :], src[g.value]).then_inc(x_in[k][g.parity], 16)

            def pieces(g):
                for k in range(PIECES):
                    if k == 3:
                        sp.wait_ge(h_ready[0], g.value)
                        load_rows(5, x_rows, g)
                    slot = k % ADJ_RING
                    sp.wait_ge(adj_binary, g.value * PIECES + (k + 1 - ADJ_RING))
                    sp.dma_start(adj_int[:, slot, :, :], adj_pieces[g.value, k]).then_inc(adj_in[slot], 16)

            def pieces_first():
                g = Group(0, 0)
                load_rows(5, x_rows, g)
                for k in range(PIECES):
                    slot = k % ADJ_RING
                    if k >= ADJ_RING:
                        sp.wait_ge(adj_binary, k + 1 - ADJ_RING)
                    sp.dma_start(adj_int[:, slot, :, :], adj_pieces[0, k]).then_inc(adj_in[slot], 16)

            pieces_first()
            pieces(Group(0, 1))
            with sp.Fori(1, GROUPS // 2) as p:
                pieces(Group(p, 0))
                pieces(Group(p, 1))

            for k in range(4):
                src = [x_rows, xs_rows, xs_rows, x3_rows][k]
                dst = [xs_rows, xs_rows, x3_rows, out_rows][k]
                if k == 0:
                    sp.wait_ge(h_ready[0], GROUPS)
                load_rows(k, src, Group(0, 0))
                if k == 2:
                    sp.wait_ge(wh_ready[2], GROUPS)
                    sp.dma_start(wh2.rearrange("(t p) f -> p t f", p=P), wh[:, :, :])\
                        .then_inc(redo_stored, 16)

                def store(g, load_next):
                    sp.wait_ge(x_new[k], g.value + 1)
                    sp.dma_start(dst[g.value], xnew[:, :, :]).then_inc(x_out[k][g.parity], 16)
                    if load_next:
                        sp.wait_ge(x_out[k][g.parity], g.half * 16 + 16)
                        load_rows(k, src, Group(g.half + g.parity, 1 - g.parity))

                with sp.Fori(0, GROUPS // 2 - 1) as p:
                    store(Group(p, 0), True)
                    store(Group(p, 1), True)
                store(Group(GROUPS // 2 - 1, 0), True)
                store(Group(GROUPS // 2 - 1, 1), False)
                for b in range(2):
                    sp.wait_ge(x_out[k][b], 16 * (GROUPS // 2))
                if k == 2:
                    sp.wait_ge(redo_known, 1)
                    groups = sp.value_load(redo_groups[0:1, 0:1], min_val=1, max_val=GROUPS)
                    with sp.Fori(0, groups) as p:
                        g = RedoGroup(p)
                        sp.wait_ge(redo_stored, g.value * 16 + 16)
                        load_rows(REDO, xs_rows, g)
                        sp.wait_ge(row_done[1], g.value * 2 + 2)
                        sp.dma_start(wh_rows[:, :, :], wh2_rows[g.value]).then_inc(wh_rows_in, 16)
                        sp.wait_ge(x_new[REDO], g.value + 1)
                        sp.dma_start(x3_rows[g.value], xnew[:, :, :]).then_inc(redo_stored, 16)
                    sp.wait_ge(redo_stored, groups * 16 + 16)

        @block.gpsimd
        def _(pool):
            nc.gpsimd.memset(ident[:, :], 0.0).then_inc(consts_ready, 1)
            nc.gpsimd.memset(packer[:, :, :], 0.0).then_inc(consts_ready, 1)
            nc.gpsimd.memset(ones[:, :], 1.0).then_inc(consts_ready, 1)
            nc.gpsimd.memset(nth[:, :], 1.0 / N).then_inc(consts_ready, 1)
            pool.wait_ge(consts_ready, 4)
            nc.gpsimd.affine_select(out=ident[:, :], in_=ident[:, :], compare_op=ALU.not_equal, fill=1.0,
                                    base=0, pattern=[[-1, P]], channel_multiplier=1).then_inc(consts_ready, 1)
            step = 5
            for b in range(BLOCKS):
                for m in range(4):
                    nc.gpsimd.affine_select(out=packer[:, b, :], in_=packer[:, b, :], compare_op=ALU.not_equal,
                                            fill=float(2 ** (4 * b + m)), base=-WORDS * m,
                                            pattern=[[-1, WORDS]], channel_multiplier=1).then_inc(consts_ready, 1)
                    step += 1
                    pool.wait_ge(consts_ready, step)
            for k, to in enumerate([S[:, :], S[:, :], S[:, :], found[:, 0:1], found[:, 1:2], S[:, :]]):
                pool.wait_ge(smax_ready, k + 1)
                nc.gpsimd.partition_all_reduce(to, smax[:, :], P, RMAX).then_inc(S_ready, 1)

        @block.vector
        def _(dve):
            edge = Chain(dve, edge_chain)
            LN_STEPS = 9

            def stats_of(k, xt, g):
                ln = Chain(dve, ln_chain[k])
                ln.at(g.value * LN_STEPS)
                for b in range(BLOCKS):
                    last = nc.vector.bn_stats(stats[:, b, :], xt[:, b, :])
                ln(last)
                nc.vector.tensor_tensor(mean2[:, :], stats[:, :, 1], stats[:, :, 4], ALU.add)
                nc.vector.tensor_tensor(ve[:, :], stats[:, :, 2], stats[:, :, 5], ALU.add)
                ln(nc.vector.tensor_tensor(rt[:, :], stats[:, :, 1], stats[:, :, 4], ALU.subtract))
                ln(nc.vector.tensor_tensor(rt[:, :], rt[:, :], rt[:, :], ALU.mult))
                ln(nc.vector.scalar_tensor_tensor(ve[:, :], rt[:, :], F / 4.0, ve[:, :], ALU.mult, ALU.add))
                nc.vector.tensor_scalar(ve[:, :], ve[:, :], 1.0 / F, EPS, ALU.mult, ALU.add)\
                    .then_inc(var_ready[k], 1)

            def scales_of(k, g):
                ln = Chain(dve, ln_chain[k])
                ln.at(g.value * LN_STEPS + 4)
                dve.wait_ge(sd_ready[k], g.value + 1)
                ln(nc.vector.reciprocal(rs[:, :], sd[:, :]))
                ln(nc.vector.tensor_tensor(rt[:, :], rs[:, :], rs[:, :], ALU.mult))
                ln(nc.vector.tensor_tensor(rt[:, :], rt[:, :], ve[:, :], ALU.mult))
                ln(nc.vector.tensor_scalar(rt[:, :], rt[:, :], -0.5, 1.5, ALU.mult, ALU.add))
                ln(nc.vector.tensor_tensor(rs[:, :], rs[:, :], rt[:, :], ALU.mult))
                assert ln.n == LN_STEPS - 4
                nc.vector.scalar_tensor_tensor(nm[:, :], mean2[:, :], -0.5, rs[:, :], ALU.mult, ALU.mult)\
                    .then_inc(norm_ready[k], 1)

            dve.wait_ge(consts_ready, CONSTS)

            def binary(g, first):
                for k in range(PIECES):
                    slot = k % ADJ_RING
                    dve.wait_ge(adj_in[slot], (g.value * (PIECES // ADJ_RING) + (k // ADJ_RING + 1)) * 16)
                    if not first or k >= ADJ_RING:
                        dve.wait_ge(adj_packed, g.value * PIECES + (k + 1 - ADJ_RING))
                    nc.vector.tensor_scalar(adj_bf[:, slot, :, :], adj_int[:, slot, :, :], 0, None, ALU.is_gt)\
                        .then_inc(adj_binary, 1)
                    if k == 4:
                        dve.wait_ge(x_in[5][g.parity], g.half * 16 + 16)
                        stats_of(0, xin[:, :, :], g)
                    if k == 8:
                        scales_of(0, g)

            binary(Group(0, 0), True)
            binary(Group(0, 1), False)
            with dve.Fori(1, GROUPS // 2) as p:
                binary(Group(p, 0), False)
                binary(Group(p, 1), False)
            dve.wait_ge(adj_packed, GROUPS * PIECES)

            def diagonal(sw, g, n):
                if n < rows_of[sw]:
                    col = [r, tau][n]
                    before = rows_of[sw] * g.value + (groups_before[sw] + n)
                    if (n == 1 if sw == REDO else not isinstance(before, int) or before > 0):
                        dve.wait_ge(row_done[own[sw]], before)
                    for b in range(BLOCKS):
                        last = nc.vector.tensor_scalar(diag[:, b, :], ident[:, :],
                                                       col[:, bass.ds(g.value * BLOCKS + b, 1)], None, ALU.mult)
                    last.then_inc(diag_ready[own[sw]], 1)

            def start_of_layer(k):
                dve.wait_ge(wh_ready[k], GROUPS)
                nc.vector.tensor_reduce(smax[:, :], s[:, 1, :], AX.X, ALU.max).then_inc(smax_ready, 1)
                if k == 2:
                    edge(nc.vector.tensor_reduce(t1[:, :], wh[:, :, :], AX.X, ALU.add))
                    edge(nc.vector.tensor_scalar(valid[:, :], t1[:, :], 0.0, None, ALU.not_equal))
                    edge(nc.vector.tensor_copy(validb[:, :], valid[:, :]))
                    nc.vector.tensor_scalar(sbig[:, :], s[:, 1, :], BIG, None, ALU.mult)
                    edge(nc.vector.tensor_copy(s1_of_2[:, :], s[:, 0, :]))
                dve.wait_ge(S_ready, k + 1 if k < 3 else 6)
                first = nc.vector.tensor_scalar(shift[:, 0:1], S[:, :], ALPHA - 1.0, None, ALU.mult)
                if k == 0:
                    first.then_inc(acc_free[0], 1)
                nc.vector.tensor_scalar(shift[:, 1:2], S[:, :], -ALPHA, None, ALU.mult)
                nc.vector.tensor_scalar(t2[:, :], s[:, 0, :], S[:, 0:1], 0.0, ALU.add, ALU.max)\
                    .then_inc(shift_ready, 1)
                dve.wait_ge(exps_ready, k + 1)
                if k == 2:
                    edge(nc.vector.tensor_tensor(D[:, :], D[:, :], valid[:, :], ALU.mult))
                diagonal(k, Group(0, 0), 0)
                nc.vector.tensor_copy(vals[:, :, F], D[:, :])
                for c in range(CHUNKS):
                    t = slice(c * JC, (c + 1) * JC)
                    nc.vector.tensor_tensor(vals[:, t, 0:F], wh[:, t, :],
                                            D[:, t].rearrange("p (t o) -> p t o", o=1).broadcast_to([P, JC, F]),
                                            ALU.mult).then_inc(vals_ready, 1)
                if k != 2:
                    dve.wait_ge(mean_done, mean_index[k] + 1)
                    edge(nc.vector.tensor_copy(mean[:, :], ps_s[:, 128:128 + F]))

            def thresholds():
                nc.vector.tensor_reduce(least[:, 0:1], sbig[:, :], AX.X, ALU.min)
                for n in range(GROUPS):
                    last = nc.vector.memset(number[:, n * BLOCKS:(n + 1) * BLOCKS], float(n + 1))
                edge(last)
                nc.vector.tensor_scalar(smax[:, :], least[:, 0:1], -1.0 / BIG, None, ALU.mult).then_inc(smax_ready, 1)
                edge(nc.vector.tensor_scalar(t1[:, :], den[:, :], THR / MASK_VALUE * 2.0 ** LN_SHIFT,
                                             2.0 ** -60, ALU.mult, ALU.max))
                nc.vector.tensor_scalar(t2[:, :], s1_of_2[:, :], S[:, 0:1], None, ALU.add).then_inc(log_arg, 1)
                dve.wait_ge(log_ready, 1)
                edge(nc.vector.scalar_tensor_tensor(t2[:, :], t2[:, :], ALPHA, t2[:, :], ALU.mult, ALU.max))
                edge(nc.vector.scalar_tensor_tensor(t1[:, :], t1[:, :], -LN_SHIFT * float(np.log(2.0)), t2[:, :],
                                                    ALU.add, ALU.add))
                edge(nc.vector.scalar_tensor_tensor(t1[:, :], t1[:, :], 1.0 / ALPHA, t1[:, :], ALU.mult, ALU.min))
                edge(nc.vector.tensor_tensor(tau[:, :], t1[:, :], s1_of_2[:, :], ALU.subtract))
                dve.wait_ge(S_ready, 4)
                edge(nc.vector.tensor_scalar(least[:, 1:2], found[:, 0:1], -1.0, None, ALU.mult))
                edge(nc.vector.scalar_tensor_tensor(t1[:, :], tau[:, :], least[:, 1:2], number[:, :],
                                                    ALU.is_ge, ALU.mult))
                nc.vector.tensor_reduce(smax[:, :], t1[:, :], AX.X, ALU.max).then_inc(smax_ready, 1)
                dve.wait_ge(S_ready, 5)
                nc.vector.tensor_scalar(redo_groups[:, :], found[:, 1:2], 1.0, None, ALU.max)\
                    .then_inc(redo_known, 1)
                dve.wait_ge(redo_known, 1)

            def column(t, i):
                return t[:, i:i + 1]

            def chunk(sw, g, c):
                kind = SWEEPS[sw][1]
                done = (g.value + groups_before[sw]) * KT + c * JC
                buf = c % 2
                if kind == "counted":
                    if not isinstance(done, int) or done >= 2 * JC:
                        dve.wait_ge(q_used[own[sw]], done - JC)
                for b in range(16):
                    op, amount = (ALU.logical_shift_left, 14 - b) if b <= 14 else (ALU.logical_shift_right, 1)
                    last = nc.vector.tensor_scalar(
                        mask[:, buf, :, b * WORDS:(b + 1) * WORDS],
                        bits[:, g.value, c * JC:(c + 1) * JC, :], amount, ONE, op, ALU.bitwise_and)
                last.then_inc(mask_ready[own[sw]], 1)
                dve.wait_ge(mask_ready[own[sw]], (g.value + groups_before[sw]) * CHUNKS + (c + 1))
                for j in range(JC):
                    if kind == "kept" and j % 2 == 0:
                        t = g.value * (KT // 2) + (c * JC + j) // 2
                        dve.wait_ge(keep_ready, t + 1)
                        pair = mask_bf[:, buf, j:j + 2, :]
                        nc.vector.tensor_tensor(pair, pair, keep[:, ((c * JC + j) // 2) % VRING, :, :], ALU.min)\
                            .then_inc(mask_kept, 1)
                        dve.wait_ge(mask_kept, t + 1)
                    tile = done + j
                    if (c * JC + j >= RING if sw == REDO else not isinstance(tile, int) or tile >= RING):
                        dve.wait_ge(q_used[own[sw]], tile + (1 - RING))
                    nc.vector.scalar_tensor_tensor(
                        q[:, j % RING, :], rrow[:, g.parity, :], column(R, c * JC + j), mask_bf[:, buf, j, :],
                        ALU.max, ALU.mult).then_inc(q_ready[own[sw]], 1)

            OUT_STEPS = {"full": 5, "counted": 6, "kept": 2}

            def outputs(sw, g):
                k, kind = SWEEPS[sw]
                a = acc[g.parity]
                chain = Chain(dve, out_chain[sw])
                chain.at(g.value * OUT_STEPS[kind])
                dve.wait_ge(q_used[own[sw]], (g.value + (groups_before[sw] + 1)) * KT)
                cols = bass.ds(g.value * BLOCKS, BLOCKS)
                dve.wait_ge(x_in[sw][g.parity], g.half * 16 + 16)
                num = a[:, :, 0:2 * (F + 1)].rearrange("p a (b f) -> p a b f", b=2)[:, :, :, 0:F]
                o4 = o[:, :, :].rearrange("p (a b) f -> p a b f", a=2)
                if kind != "kept":
                    dens = a[:, :, F:2 * (F + 1):F + 1]
                    d22 = den4[:, :].rearrange("p (a b) -> p a b", a=2)
                    chain(nc.vector.tensor_copy(d22, dens))
                    chain(nc.vector.tensor_scalar(none4[:, :], den4[:, :], 0.0, None, ALU.is_equal))
                    chain(nc.vector.tensor_tensor(den4[:, :], den4[:, :], none4[:, :], ALU.add))
                    chain(nc.vector.reciprocal(rec4[:, :], den4[:, :]))
                if kind == "counted":
                    counts = a[:, 0, 2 * (F + 1):2 * (F + 1) + BLOCKS]
                    nc.vector.tensor_tensor(den[:, cols], den4[:, :], none4[:, :], ALU.subtract)
                    chain(nc.vector.scalar_tensor_tensor(rec4[:, :], counts, 1.0 / MASK_VALUE, rec4[:, :],
                                                         ALU.mult, ALU.mult))
                    nc.vector.tensor_copy(kappa[:, cols], rec4[:, :])
                if kind == "kept":
                    chain(nc.vector.tensor_copy(rec4[:, :], kappa[:, cols]))
                scale = rec4[:, :]
                scale = scale.rearrange("p (a b o) -> p a b o", a=2, o=1).broadcast_to([P, 2, 2, F])
                ins = nc.vector.tensor_tensor(o4, num, scale, ALU.mult)
                ins.then_inc(acc_free[own[sw]], 1)
                dve.wait_ge(acc_free[own[sw]], g.value + (groups_before[sw] + (1 if sw == REDO else 2)))
                if kind == "full":
                    for b in range(BLOCKS):
                        last = nc.vector.scalar_tensor_tensor(o[:, b, :], mean[:, :], none4[:, b:b + 1], o[:, b, :],
                                                              ALU.mult, ALU.add)
                    chain(last)
                else:
                    own_rows = wh[:, cols, :]
                    if sw == REDO:
                        dve.wait_ge(wh_rows_in, g.value * 16 + 16)
                        own_rows = wh_rows[:, :, :]
                    chain(nc.vector.tensor_tensor(o[:, :, :], o[:, :, :], own_rows, ALU.add))
                if k == 0:
                    nc.vector.tensor_tensor(xnew[:, :, :], xin[:, :, :], o[:, :, :], ALU.add)\
                        .then_inc(x_new[sw], 1)
                else:
                    nc.vector.tensor_scalar(e[:, :, :], o[:, :, :], 0.0, None, ALU.min).then_inc(elu_arg[sw], 1)

            def new_rows(sw, g):
                k, kind = SWEEPS[sw]
                xn = xnew[:, :, :]
                if k > 0:
                    nc.vector.scalar_tensor_tensor(o[:, :, :], o[:, :, :], 0.0, xin[:, :, :],
                                                   ALU.max, ALU.add).then_inc(elu_arg[sw], 1)
                    dve.wait_ge(elu_arg[sw], g.value * 2 + 2)
                    dve.wait_ge(elu_exp[sw], g.value + 1)
                    nc.vector.scalar_tensor_tensor(xn, e[:, :, :], -1.0, o[:, :, :], ALU.add, ALU.add)\
                        .then_inc(x_new[sw], 1)
                dve.wait_ge(x_new[sw], g.value + 1)
                if k < 3:
                    stats_of(next_projection(sw), xn, g)

            def rows_scaled(sw, g):
                k, kind = SWEEPS[sw]
                if k < 3:
                    scales_of(next_projection(sw), g)

            def body(sw):
                def group(g, before, more):
                    n = rows_of[sw] * g.value + (groups_before[sw] + rows_of[sw])
                    dve.wait_ge(row_ready[own[sw]], n)
                    for c in range(CHUNKS):
                        chunk(sw, g, c)
                        if c == 0:
                            if before:
                                outputs(sw, before)
                            if more:
                                diagonal(sw, Group(g.half + g.parity, 1 - g.parity), 0)
                        if before and c == 1:
                            new_rows(sw, before)
                        if before and c == 2:
                            rows_scaled(sw, before)
                        if more and c == 2:
                            diagonal(sw, Group(g.half + g.parity, 1 - g.parity), 1)
                return group

            def last_tail(sw):
                def tail(g):
                    outputs(sw, g)
                    new_rows(sw, g)
                    rows_scaled(sw, g)
                return tail

            for sw in MAIN:
                start_of_layer(sw)
                every_group(dve, body(sw), last_tail(sw))
                if sw == 2:
                    thresholds()
                    with dve.Fori(0, dve.value_load(redo_groups[0:1, 0:1], min_val=1, max_val=GROUPS)) as p:
                        g = RedoGroup(p)
                        diagonal(REDO, g, 0)
                        diagonal(REDO, g, 1)
                        body(REDO)(g, None, False)
                        last_tail(REDO)(g)
                        dve.wait_ge(wh_ready[REPROJECT], g.value + 1)

        @block.tensor
        def _(pe):
            def transposes(k, g):
                pe.wait_ge(h_ready[k], g.value + 1)
                for b in range(BLOCKS):
                    last = nc.tensor.transpose(ps_tr[:, b * P:(b + 1) * P], h[:, b, :], ident[:, :])
                last.then_inc(tr_done[k], 1)

            def project(k, g):
                pe.wait_ge(hT_ready[k], g.value + 1)
                for b in range(BLOCKS):
                    nc.tensor.matmul(ps_wh[:, b * F:(b + 1) * F], hT[:, b, :], w_sb[:, layer_of(k), :], start=True,
                                     stop=True)
                for b in range(BLOCKS):
                    last = nc.tensor.matmul(ps_s[:, 2 * b:2 * b + 2], hT[:, b, :], wa[:, layer_of(k), :],
                                            start=True, stop=True)
                last.then_inc(wh_done[k], 1)

            pe.wait_ge(weights_in, 16 * 12)
            pe.wait_ge(consts_ready, CONSTS)
            for k in range(4):
                last = nc.tensor.transpose(ps_tr[:, k * P:(k + 1) * P], w_sb[:, k, :], ident[:, :])
            last.then_inc(wT_done, 1)
            pe.wait_ge(wT_copied, 1)
            for k in range(4):
                last = nc.tensor.matmul(ps_s[:, 2 * k:2 * k + 2], wT[:, k, :], a_sb[:, k, :], start=True, stop=True)
            last.then_inc(wa_done, 1)
            pe.wait_ge(wa_copied, 1)

            def pack(g, first):
                for k in range(PIECES):
                    quarter, slot = k // 4, k % ADJ_RING
                    if not first and k % 4 == 0:
                        pe.wait_ge(bits_ready, g.value * 4 + (quarter - 3))
                    pe.wait_ge(adj_binary, g.value * PIECES + (k + 1))
                    for t in range(AJ):
                        at = ((k % 4) * AJ + t) * WORDS
                        for b in range(BLOCKS):
                            last = nc.tensor.matmul(pack_bank[quarter][:, at:at + WORDS],
                                                    adj_bf[:, slot, b, t * P:(t + 1) * P], packer[:, b, :],
                                                    start=(b == 0), stop=(b == BLOCKS - 1))
                    last.then_inc(adj_packed, 1)
                    if k == 12:
                        transposes(0, g)
                    if k == 14:
                        project(0, g)

            pack(Group(0, 0), True)
            pack(Group(0, 1), False)
            with pe.Fori(1, GROUPS // 2) as p:
                pack(Group(p, 0), False)
                pack(Group(p, 1), False)

            def spread(sw, g, n):
                if n < rows_of[sw]:
                    done = rows_of[sw] * g.value + (groups_before[sw] + n)
                    pe.wait_ge(diag_ready[own[sw]], done + 1)
                    if (n == 1 if sw == REDO else not isinstance(done, int) or done > 0):
                        pe.wait_ge(row_ready[own[sw]], done)
                    for b in range(BLOCKS):
                        last = nc.tensor.matmul(ps_bc[:, b * P:(b + 1) * P], ones[:, :], diag[:, b, :],
                                                start=True, stop=True)
                    last.then_inc(row_done[own[sw]], 1)

            def mean_row(k):
                pe.wait_ge(wh_ready[k], GROUPS)
                for t in range(KT):
                    last = nc.tensor.matmul(ps_s[:, 128:128 + F], nth[:, :], wh[:, t, :],
                                            start=(t == 0), stop=(t == KT - 1))
                last.then_inc(mean_done, 1)

            def sweep_chunk(sw, g, c, middle):
                kind = SWEEPS[sw][1]
                a = acc[g.parity]
                for j in range(JC):
                    t = c * JC + j
                    pe.wait_ge(q_ready[own[sw]], (g.value + groups_before[sw]) * KT + (t + 1))
                    for b in range(BLOCKS):
                        at = (b % 2) * (F + 1)
                        last = nc.tensor.matmul(a[:, b // 2, at:at + F + 1], q[:, j % RING, b * P:(b + 1) * P],
                                                vals[:, t, :], start=(t == 0 and b % 2 == 0), stop=(t == KT - 1),
                                                skip_group_check=True)
                    if kind == "counted":
                        for b in range(BLOCKS):
                            at = 2 * (F + 1) + b
                            last = nc.tensor.matmul(a[:, 0, at:at + 1], mask_bf[:, c % 2, j, b * P:(b + 1) * P],
                                                    validb[:, t:t + 1], start=False, stop=(t == KT - 1),
                                                    skip_group_check=True)
                    last.then_inc(q_used[own[sw]], 1)
                    if j == JC // 2 - 1:
                        middle()

            def body(sw):
                k, kind = SWEEPS[sw]
                projects = k < 3

                def group(g, before, more):
                    if sw != REDO and (not isinstance(g.value, int) or g.value + groups_before[sw] > 0):
                        pe.wait_ge(acc_free[own[sw]], g.value + groups_before[sw])
                    for c in range(CHUNKS):
                        def middle():
                            if c == 3 and more:
                                spread(sw, Group(g.half + g.parity, 1 - g.parity), 1)
                            if c == 3 and before and projects:
                                transposes(k + 1, before)
                        sweep_chunk(sw, g, c, middle)
                        if c == 1 and more:
                            spread(sw, Group(g.half + g.parity, 1 - g.parity), 0)
                        if c == 3 and before and projects:
                            project(k + 1, before)
                return group

            def last_tail(sw):
                def tail(g):
                    if SWEEPS[sw][0] < 3:
                        transposes(next_projection(sw), g)
                        project(next_projection(sw), g)
                return tail

            for sw in MAIN:
                spread(sw, Group(0, 0), 0)
                if sw != 2:
                    mean_row(sw)
                pe.wait_ge(vals_ready, CHUNKS * (sw + 1))
                every_group(pe, body(sw), last_tail(sw))
                if sw == 2:
                    pe.wait_ge(redo_known, 1)
                    with pe.Fori(0, pe.value_load(redo_groups[0:1, 0:1], min_val=1, max_val=GROUPS)) as p:
                        g = RedoGroup(p)
                        spread(REDO, g, 0)
                        spread(REDO, g, 1)
                        body(REDO)(g, None, False)
                        last_tail(REDO)(g)
                        pe.wait_ge(wh_ready[REPROJECT], g.value + 1)

        @block.scalar
        def _(act):
            act.wait_ge(wT_done, 1)
            nc.scalar.activation(wT[:, :, :], ps_tr[:, :].rearrange("p (k f) -> p k f", k=4), ACT.Copy)\
                .then_inc(wT_copied, 1)
            act.wait_ge(wa_done, 1)
            nc.scalar.activation(wa[:, :, :], ps_s[:, 0:8].rearrange("p (k c) -> p k c", k=4), ACT.Copy)\
                .then_inc(wa_copied, 1)

            def deviations(k, g):
                act.wait_ge(var_ready[k], g.value + 1)
                nc.scalar.activation(sd[:, :], ve[:, :], ACT.Sqrt).then_inc(sd_ready[k], 1)

            def normalised(k, xt, g):
                act.wait_ge(norm_ready[k], g.value + 1)
                for b in range(BLOCKS):
                    last = nc.scalar.activation(h[:, b, :], xt[:, b, :], ACT.Relu, bias=nm[:, b:b + 1],
                                                scale=rs[:, b:b + 1])
                last.then_inc(h_ready[k], 1)

            def copy_hT(k, g):
                act.wait_ge(tr_done[k], g.value + 1)
                nc.scalar.activation(hT[:, :, :], ps_tr[:, :].rearrange("p (b f) -> p b f", b=BLOCKS), ACT.Copy)\
                    .then_inc(hT_ready[k], 1)

            def copy_wh(k, g):
                act.wait_ge(wh_done[k], g.value + 1)
                cols = bass.ds(g.value * BLOCKS, BLOCKS)
                nc.scalar.activation(wh[:, cols, :], ps_wh[:, :].rearrange("p (b f) -> p b f", b=BLOCKS), ACT.Copy)
                nc.scalar.activation(s[:, :, cols], ps_s[:, 0:2 * BLOCKS].rearrange("p (b c) -> p c b", c=2),
                                     ACT.Copy).then_inc(wh_ready[k], 1)

            def words(g):
                for quarter in range(4):
                    act.wait_ge(adj_packed, g.value * PIECES + 4 * (quarter + 1))
                    nc.scalar.activation(
                        bits[:, g.value, quarter * JC:(quarter + 1) * JC, :],
                        pack_bank[quarter].rearrange("p (t n) -> p t n", t=JC), ACT.Copy).then_inc(bits_ready, 1)
                    if quarter == 1:
                        deviations(0, g)
                        normalised(0, xin[:, :, :], g)
                    if quarter == 2:
                        copy_hT(0, g)
                copy_wh(0, g)

            with act.Fori(0, GROUPS // 2) as p:
                words(Group(p, 0))
                words(Group(p, 1))

            def copy_rows(sw, g, n):
                if n < rows_of[sw]:
                    row = [rrow[:, g.parity, :], taurow[:, :]][n]
                    act.wait_ge(row_done[own[sw]], rows_of[sw] * g.value + (groups_before[sw] + n + 1))
                    nc.scalar.activation(row, ps_bc[:, :], ACT.Copy).then_inc(row_ready[own[sw]], 1)

            def elu_exp_of(sw, g):
                act.wait_ge(elu_arg[sw], g.value * 2 + 1)
                nc.scalar.activation(e[:, :, :], e[:, :, :], ACT.Exp).then_inc(elu_exp[sw], 1)

            def keep_tile(g, t):
                n = g.value * (KT // 2) + t
                if t >= VRING:
                    act.wait_ge(mask_kept, n + (1 - VRING))
                for j in range(2):
                    last = nc.scalar.activation(keep[:, t % VRING, j, :], taurow[:, :], ACT.Relu,
                                                scale=-BIG, bias=sbig[:, 2 * t + j:2 * t + j + 1])
                last.then_inc(keep_ready, 1)

            def body(sw):
                def group(g, before, more):
                    if before and sw > 0:
                        elu_exp_of(sw, before)
                    if more:
                        copy_rows(sw, Group(g.half + g.parity, 1 - g.parity), 0)
                    if before and sw < 3:
                        deviations(sw + 1, before)
                        normalised(sw + 1, xnew[:, :, :], before)
                        copy_hT(sw + 1, before)
                        copy_wh(sw + 1, before)
                return group

            def last_tail(sw):
                k, kind = SWEEPS[sw]

                def tail(g):
                    if k > 0:
                        elu_exp_of(sw, g)
                    if k < 3:
                        to = next_projection(sw)
                        deviations(to, g)
                        normalised(to, xnew[:, :, :], g)
                        copy_hT(to, g)
                        copy_wh(to, g)
                return tail

            for sw in MAIN:
                act.wait_ge(shift_ready, sw + 1)
                nc.scalar.activation(R[:, :], s[:, 1, :], ACT.Exp, scale=1.0 - ALPHA, bias=shift[:, 0:1])
                nc.scalar.activation(D[:, :], s[:, 1, :], ACT.Exp, scale=ALPHA, bias=shift[:, 1:2])
                nc.scalar.activation(r[:, :], t2[:, :], ACT.Exp, scale=ALPHA - 1.0).then_inc(exps_ready, 1)
                copy_rows(sw, Group(0, 0), 0)
                if sw == 2:
                    act.wait_ge(redo_stored, 16)
                every_group(act, body(sw), last_tail(sw))
                if sw == 2:
                    act.wait_ge(log_arg, 1)
                    nc.scalar.activation(t1[:, :], t1[:, :], ACT.Ln).then_inc(log_ready, 1)
                    act.wait_ge(redo_known, 1)
                    with act.Fori(0, act.value_load(redo_groups[0:1, 0:1], min_val=1, max_val=GROUPS)) as p:
                        g = RedoGroup(p)
                        copy_rows(REDO, g, 0)
                        copy_rows(REDO, g, 1)
                        act.wait_ge(row_ready[1], g.value * 2 + 2)
                        for t in range(KT // 2):
                            keep_tile(g, t)
                        last_tail(REDO)(g)


_WS = [f"L{k}_gnn_W" for k in range(4)]
_AS = [f"L{k}_gnn_a" for k in range(4)]


def kernel(**inputs):
    import numpy as _np
    import concourse.bacc as _bacc
    from concourse import mybir as _mybir
    from concourse.bass_utils import run_bass_kernel_spmd as _run

    nc = _bacc.Bacc("TRN2", target_bir_lowering=False, num_devices=1)
    arrays, aps = {}, {}
    for name in ["x", "adj"] + _WS + _AS:
        a = _np.ascontiguousarray(inputs[name])
        arrays[f"in_{name}_dram"] = a
        aps[name] = nc.dram_tensor(f"in_{name}_dram", a.shape, _mybir.dt.from_np(a.dtype), kind="ExternalInput").ap()
    out = nc.dram_tensor("out_0_dram", (N, F), F32, kind="ExternalOutput").ap()
    build(nc, aps["x"], aps["adj"], [aps[n] for n in _WS], [aps[n] for n in _AS], out)
    r = _run(nc, [arrays], core_ids=[0])
    return r.results[0]["out_0_dram"]
```

```python
from contextlib import ExitStack

import numpy as np

import concourse.bass as bass
from concourse import mybir

P = 128
F = 128
N = 8192
BLOCKS = 4
W = P * BLOCKS
GROUPS = N // W
KT = N // P
CHUNKS = 4
JC = KT // CHUNKS
WORDS = W // 16
RING = 8
AJ = 2
PIECES = KT // AJ
QP = PIECES // CHUNKS
ADJ_RING = 4
BIN_RING = 2
STEEP = 2.0 ** 20
VRING = 2
ONE = 0x4000
MASK_VALUE = 2.0
ALPHA = 0.2
EPS = 1e-5
THR = 1e-4
BIG = 2.0 ** 60
LIFT = 2.0 ** 64
LN_SHIFT = 43

F32 = mybir.dt.float32
BF16 = mybir.dt.bfloat16
U16 = mybir.dt.uint16
I32 = mybir.dt.int32
ALU = mybir.AluOpType
ACT = mybir.ActivationFunctionType
AX = mybir.AxisListType
RMAX = bass.bass_isa.ReduceOp.max

SWEEPS = [(0, "full"), (1, "full"), (2, "counted"), (3, "full"), (2, "kept")]
REDO = 4
MAIN = range(4)
REPROJECT = 4


def next_projection(sw):
    return REPROJECT if sw == REDO else sw + 1


def layer_of(projection):
    return min(projection, 3)


class Group:

    def __init__(self, half, parity):
        self.half, self.parity = half, parity
        self.value = half * 2 + parity


def every_group(eng, body, tail):
    body(Group(0, 0), None, True)
    with eng.Fori(0, GROUPS // 2 - 1) as p:
        body(Group(p, 1), Group(p, 0), True)
        body(Group(p + 1, 0), Group(p, 1), True)
    body(Group(GROUPS // 2 - 1, 1), Group(GROUPS // 2 - 1, 0), False)
    tail(Group(GROUPS // 2 - 1, 1))


def every_quad(eng, body):
    body(0, False)
    with eng.Fori(1, CHUNKS - 1) as m:
        body(m, False)
    body(CHUNKS - 1, True)


def after(g):
    return Group(g.half + g.parity, 1 - g.parity)


class RedoGroup:

    def __init__(self, value):
        self.value = self.half = value
        self.parity = 0


class Chain:

    def __init__(self, eng, sem):
        self.eng, self.sem, self.base, self.n = eng, sem, 0, 0

    def at(self, base):
        self.base, self.n = base, 0

    def __call__(self, ins):
        self.n += 1
        ins.then_inc(self.sem, 1)
        self.eng.wait_ge(self.sem, self.base + self.n)


def build(nc, x, adj, ws, avs, out):
    x_rows = x.rearrange("(g q p) f -> g p q f", q=BLOCKS, p=P)
    out_rows = out.rearrange("(g q p) f -> g p q f", q=BLOCKS, p=P)
    xs = nc.dram_tensor("x_between_layers", (N, F), F32).ap()
    xs_rows = xs.rearrange("(g q p) f -> g p q f", q=BLOCKS, p=P)
    x3 = nc.dram_tensor("x_of_layer_3", (N, F), F32).ap()
    x3_rows = x3.rearrange("(g q p) f -> g p q f", q=BLOCKS, p=P)
    wh2 = nc.dram_tensor("wh_of_layer_2", (N, F), F32).ap()
    wh2_rows = wh2.rearrange("(g q p) f -> g p q f", q=BLOCKS, p=P)
    adj_pieces = adj.rearrange("(g q p) (k c) -> g k p q c", q=BLOCKS, p=P, c=AJ * P)

    with ExitStack() as ctx:
        def sb(name, shape, dt):
            return ctx.enter_context(nc.sbuf_tensor(name, shape, dt))

        def ps(name, shape):
            return ctx.enter_context(nc.psum_tensor(name, shape, F32))

        def sem(name):
            return ctx.enter_context(nc.semaphore(name))

        bits = sb("bits", [P, GROUPS, KT, WORDS], U16)
        vals = sb("vals", [P, KT, F + 1], F32)
        wh = sb("wh", [P, KT, F], F32)
        mask = sb("mask", [P, 2, JC, W], U16)
        q = sb("q", [P, RING, W], F32)
        rrow = sb("rrow", [P, 2, W], F32)
        taurow = sb("taurow", [P, W], F32)
        keep = sb("keep", [P, VRING, 2, W], BF16)
        diag = sb("diag", [P, BLOCKS, P], F32)
        xin = sb("xin", [P, BLOCKS, F], F32)
        xnew = sb("xnew", [P, BLOCKS, F], F32)
        e = sb("e", [P, BLOCKS, F], F32)
        hT = sb("hT", [P, BLOCKS, F], F32)
        w_sb = sb("w_sb", [P, 4, F + 2], F32)
        a_sb = sb("a_sb", [P, 4, 2], F32)
        ident = sb("ident", [P, P], F32)
        ones = sb("ones", [P, P], F32)
        h_sum = sb("h_sum", [P, GROUPS], F32)
        h_total = sb("h_total", [P, 1], F32)
        h_mean = sb("h_mean", [P, P], F32)
        threshold = sb("threshold", [P, 1], F32)
        packer = sb("packer", [P, BLOCKS, WORDS], BF16)
        mean = sb("mean", [P, F], F32)
        s = sb("s", [P, 2, KT], F32)
        smax = sb("smax", [P, 1], F32)
        S = sb("S", [P, 1], F32)
        shift = sb("shift", [P, 2], F32)
        R = sb("R", [P, KT], F32)
        D = sb("D", [P, KT], F32)
        r = sb("r", [P, KT], F32)
        tau = sb("tau", [P, KT], F32)
        t1 = sb("t1", [P, KT], F32)
        t2 = sb("t2", [P, KT], F32)
        sbig = sb("sbig", [P, KT], F32)
        valid = sb("valid", [P, KT], F32)
        validb = sb("validb", [P, KT], BF16)
        den = sb("den", [P, KT], F32)
        s1_of_2 = sb("s1_of_2", [P, KT], F32)
        number = sb("number", [P, KT], F32)
        least = sb("least", [P, 2], F32)
        found = sb("found", [P, 2], F32)
        redo_groups = sb("redo_groups", [P, 1], I32)
        kappa = sb("kappa", [P, KT], F32)
        den4 = sb("den4", [P, BLOCKS], F32)
        none4 = sb("none4", [P, BLOCKS], F32)
        rec4 = sb("rec4", [P, BLOCKS], F32)
        stats = sb("stats", [P, BLOCKS, 6], F32)
        mean2 = sb("mean2", [P, BLOCKS], F32)
        ve = sb("ve", [P, BLOCKS], F32)
        sd = sb("sd", [P, BLOCKS], F32)
        rs = sb("rs", [P, BLOCKS], F32)
        rt = sb("rt", [P, BLOCKS], F32)
        nm = sb("nm", [P, BLOCKS], F32)

        acc = [ps(f"acc{k}", [P, 2, 512]) for k in range(2)]
        ps_bc = ps("ps_bc", [P, 512])
        ps_wh = ps("ps_wh", [P, 2, 512])
        ps_pack = ps("ps_pack", [P, 512])

        o, h, wT = xnew, e, hT
        ps_tr = ps_wh[:, 0, :]
        ps_s = ps_wh[:, 1, :]
        projected = ps_wh[:, :, 0:2 * (F + 2)].rearrange("p a (b f) -> p a b f", b=2)
        wh_rows = diag
        adj_int = mask[:, 1, :, :].rearrange("p b c -> p (b c)").bitcast(I32).rearrange(
            "p (n q c) -> p n q c", n=ADJ_RING, q=BLOCKS)
        adj_bf = keep[:, :, :, :].rearrange("p a b c -> p (a b c)").rearrange(
            "p (n q c) -> p n q c", n=BIN_RING, q=BLOCKS)
        mask_bf = mask[:, :, :, :].rearrange("p a b c -> p (a b c)").bitcast(BF16).rearrange(
            "p (a b c) -> p a b c", a=2, b=JC)

        consts_ready = sem("consts_ready")
        weights_in = sem("weights_in")
        wT_done = sem("wT_done")
        wT_copied = sem("wT_copied")
        wa_done = sem("wa_done")
        wa_copied = sem("wa_copied")
        adj_in = [sem(f"adj_in{k}") for k in range(ADJ_RING)]
        adj_binary = sem("adj_binary")
        adj_packed = sem("adj_packed")
        bits_ready = sem("bits_ready")
        mask_ready = [sem("mask_ready"), sem("redo_mask_ready")]
        q_ready = [sem("q_ready"), sem("redo_q_ready")]
        q_used = [sem("q_used"), sem("redo_q_used")]
        acc_free = [sem("acc_free"), sem("redo_acc_free")]
        diag_ready = [sem("diag_ready"), sem("redo_diag_ready")]
        row_done = [sem("row_done"), sem("redo_row_done")]
        row_ready = [sem("row_ready"), sem("redo_row_ready")]
        keep_ready = sem("keep_ready")
        mask_kept = sem("mask_kept")
        var_ready = [sem(f"var_ready{k}") for k in range(5)]
        sd_ready = [sem(f"sd_ready{k}") for k in range(5)]
        norm_ready = [sem(f"norm_ready{k}") for k in range(5)]
        h_ready = [sem(f"h_ready{k}") for k in range(5)]
        tr_done = [sem(f"tr_done{k}") for k in range(5)]
        hT_ready = [sem(f"hT_ready{k}") for k in range(5)]
        wh_done = [sem(f"wh_done{k}") for k in range(5)]
        wh_ready = [sem(f"wh_ready{k}") for k in range(5)]
        ln_chain = [sem(f"ln_chain{k}") for k in range(5)]
        out_chain = [sem(f"out_chain{k}") for k in range(5)]
        rec_ready = [sem(f"rec_ready{k}") for k in range(4)]
        elu_neg = [sem(f"elu_neg{k}") for k in range(5)]
        elu_arg = [sem(f"elu_arg{k}") for k in range(5)]
        elu_exp = [sem(f"elu_exp{k}") for k in range(5)]
        x_new = [sem(f"x_new{k}") for k in range(5)]
        x_in = [[sem(f"x_in{k}_{b}") for b in range(2)] for k in range(6)]
        x_out = [[sem(f"x_out{k}_{b}") for b in range(2)] for k in range(4)]
        smax_ready = sem("smax_ready")
        S_ready = sem("S_ready")
        h_mean_ready = sem("h_mean_ready")
        mean_done = sem("mean_done")
        shift_ready = sem("shift_ready")
        exps_ready = sem("exps_ready")
        vals_ready = sem("vals_ready")
        edge_chain = sem("edge_chain")
        log_arg = sem("log_arg")
        log_ready = sem("log_ready")
        redo_stored = sem("redo_stored")
        wh_rows_in = sem("wh_rows_in")
        redo_known = sem("redo_known")

        own = [0, 0, 0, 0, 1]
        groups_before = [k * GROUPS for k in MAIN] + [0]
        rows_of = [1, 1, 1, 1, 2]

        mean_index = {0: 0, 1: 1, 3: 2}
        CONSTS = 5 + 16

        block = ctx.enter_context(nc.Block())

        @block.sync
        def _(sp):
            for k in range(4):
                sp.dma_start(w_sb[:, k, 0:F], ws[k]).then_inc(weights_in, 16)
                for c in range(2):
                    sp.dma_start(a_sb[:, k, c:c + 1], avs[k][c * F:(c + 1) * F, :]).then_inc(weights_in, 16)

            def load_rows(k, src, g, to=xin):
                sp.dma_start(to[:, :, :], src[g.value]).then_inc(x_in[k][g.parity], 16)

            def load_piece(before, slot, g, k):
                if not isinstance(before, int) or before >= ADJ_RING:
                    sp.wait_ge(adj_binary, before + (1 - ADJ_RING))
                sp.dma_start(adj_int[:, slot, :, :], adj_pieces[g, k]).then_inc(adj_in[slot], 16)

            load_rows(5, x_rows, Group(0, 0))

            def first_loads(m, last):
                for n in range(4):
                    g = Group(m * 2 + n // 2, n % 2)
                    for j in range(2):
                        load_piece(m * QP + (2 * n + j), (2 * n + j) % ADJ_RING, 0, m * QP + (2 * n + j))
                    if not (last and n == 3):
                        if not isinstance(g.value, int) or g.value >= 1:
                            sp.wait_ge(h_ready[0], g.value)
                        load_rows(5, x_rows, after(g), [xin, xnew][1 - g.parity])

            every_quad(sp, first_loads)

            for k in range(4):
                src = [x_rows, xs_rows, xs_rows, x3_rows][k]
                dst = [xs_rows, xs_rows, x3_rows, out_rows][k]
                if k == 0:
                    sp.wait_ge(h_ready[0], GROUPS)
                load_rows(k, src, Group(0, 0))
                if k == 2:
                    sp.wait_ge(wh_ready[2], GROUPS)
                    sp.dma_start(wh2.rearrange("(t p) f -> p t f", p=P), wh[:, :, :])\
                        .then_inc(redo_stored, 16)

                def store(g):
                    sp.wait_ge(x_new[k], g.value + 1)
                    sp.dma_start(dst[g.value], xnew[:, :, :]).then_inc(x_out[k][g.parity], 16)

                def load_after(g):
                    sp.wait_ge(x_out[k][g.parity], g.half * 16 + 16)
                    load_rows(k, src, after(g))

                if k == 0:
                    def transfers(g, before, more):
                        for i in range(PIECES):
                            if before and i == 22:
                                store(before)
                            if before and i == 27:
                                load_after(before)
                            if more:
                                to = after(g)
                                load_piece(to.value * PIECES + i, i % ADJ_RING, to.value, i)

                    every_group(sp, transfers, store)
                    for b in range(2):
                        sp.wait_ge(x_out[k][b], 16 * (GROUPS // 2))
                    continue

                with sp.Fori(0, GROUPS // 2 - 1) as p:
                    for parity in range(2):
                        store(Group(p, parity))
                        load_after(Group(p, parity))
                store(Group(GROUPS // 2 - 1, 0))
                load_after(Group(GROUPS // 2 - 1, 0))
                store(Group(GROUPS // 2 - 1, 1))
                for b in range(2):
                    sp.wait_ge(x_out[k][b], 16 * (GROUPS // 2))
                if k == 2:
                    sp.wait_ge(redo_known, 1)
                    groups = sp.value_load(redo_groups[0:1, 0:1], min_val=1, max_val=GROUPS)
                    with sp.Fori(0, groups) as p:
                        g = RedoGroup(p)
                        sp.wait_ge(redo_stored, g.value * 16 + 16)
                        load_rows(REDO, xs_rows, g)
                        sp.wait_ge(row_done[1], g.value * 2 + 2)
                        sp.dma_start(wh_rows[:, :, :], wh2_rows[g.value]).then_inc(wh_rows_in, 16)
                        sp.wait_ge(x_new[REDO], g.value + 1)
                        sp.dma_start(x3_rows[g.value], xnew[:, :, :]).then_inc(redo_stored, 16)
                    sp.wait_ge(redo_stored, groups * 16 + 16)

        @block.gpsimd
        def _(pool):
            nc.gpsimd.memset(ident[:, :], 0.0).then_inc(consts_ready, 1)
            nc.gpsimd.memset(packer[:, :, :], 0.0).then_inc(consts_ready, 1)
            nc.gpsimd.memset(ones[:, :], 1.0).then_inc(consts_ready, 1)
            nc.gpsimd.memset(threshold[:, :], -STEEP / 2).then_inc(consts_ready, 1)
            pool.wait_ge(consts_ready, 4)
            nc.gpsimd.affine_select(out=ident[:, :], in_=ident[:, :], compare_op=ALU.not_equal, fill=1.0,
                                    base=0, pattern=[[-1, P]], channel_multiplier=1).then_inc(consts_ready, 1)
            step = 5
            for b in range(BLOCKS):
                for m in range(4):
                    nc.gpsimd.affine_select(out=packer[:, b, :], in_=packer[:, b, :], compare_op=ALU.not_equal,
                                            fill=float(2 ** (4 * b + m)), base=-WORDS * m,
                                            pattern=[[-1, WORDS]], channel_multiplier=1).then_inc(consts_ready, 1)
                    step += 1
                    pool.wait_ge(consts_ready, step)
            for k, to in enumerate([S[:, :], S[:, :], S[:, :], found[:, 0:1], found[:, 1:2], S[:, :]]):
                pool.wait_ge(smax_ready, k + 1)
                nc.gpsimd.partition_all_reduce(to, smax[:, :], P, RMAX).then_inc(S_ready, 1)

        @block.vector
        def _(dve):
            edge = Chain(dve, edge_chain)
            LN_STEPS = 9

            def stats_of(k, xt, g):
                ln = Chain(dve, ln_chain[k])
                ln.at(g.value * LN_STEPS)
                for b in range(BLOCKS):
                    last = nc.vector.bn_stats(stats[:, b, :], xt[:, b, :])
                ln(last)
                nc.vector.tensor_tensor(mean2[:, :], stats[:, :, 1], stats[:, :, 4], ALU.add)
                nc.vector.tensor_tensor(ve[:, :], stats[:, :, 2], stats[:, :, 5], ALU.add)
                ln(nc.vector.tensor_tensor(rt[:, :], stats[:, :, 1], stats[:, :, 4], ALU.subtract))
                ln(nc.vector.tensor_tensor(rt[:, :], rt[:, :], rt[:, :], ALU.mult))
                ln(nc.vector.scalar_tensor_tensor(ve[:, :], rt[:, :], F / 4.0, ve[:, :], ALU.mult, ALU.add))
                nc.vector.tensor_scalar(ve[:, :], ve[:, :], 1.0 / F, EPS, ALU.mult, ALU.add)\
                    .then_inc(var_ready[k], 1)

            def scales_of(k, g):
                ln = Chain(dve, ln_chain[k])
                ln.at(g.value * LN_STEPS + 4)
                dve.wait_ge(sd_ready[k], g.value + 1)
                ln(nc.vector.reciprocal(rs[:, :], sd[:, :]))
                ln(nc.vector.tensor_tensor(rt[:, :], rs[:, :], rs[:, :], ALU.mult))
                ln(nc.vector.tensor_tensor(rt[:, :], rt[:, :], ve[:, :], ALU.mult))
                ln(nc.vector.tensor_scalar(rt[:, :], rt[:, :], -0.5, 1.5, ALU.mult, ALU.add))
                ln(nc.vector.tensor_tensor(rs[:, :], rs[:, :], rt[:, :], ALU.mult))
                assert ln.n == LN_STEPS - 4
                nc.vector.scalar_tensor_tensor(nm[:, :], mean2[:, :], -0.5, rs[:, :], ALU.mult, ALU.mult)\
                    .then_inc(norm_ready[k], 1)

            dve.wait_ge(consts_ready, CONSTS)

            def first_stats(g):
                dve.wait_ge(x_in[5][g.parity], g.half * 16 + 16)
                stats_of(0, [xin, xnew][g.parity][:, :, :], g)

            first_stats(Group(0, 0))

            def first_scales(g, before, more):
                if before:
                    dve.wait_ge(h_ready[0], g.value)
                scales_of(0, g)
                if more:
                    first_stats(after(g))

            def binary(m, i):
                slot, n = i % ADJ_RING, m * QP + i
                dve.wait_ge(adj_in[slot], (m * (QP // ADJ_RING) + i // ADJ_RING) * 16 + 16)
                if not isinstance(n, int) or n >= BIN_RING:
                    dve.wait_ge(adj_packed, n + (1 - BIN_RING))
                nc.vector.tensor_scalar(adj_bf[:, i % BIN_RING, :, :], adj_int[:, slot, :, :], 0, None, ALU.is_gt)\
                    .then_inc(adj_binary, 1)

            def first_rows(m, last):
                for n in range(4):
                    g = Group(m * 2 + n // 2, n % 2)
                    first_scales(g, not isinstance(m, int) or m > 0 or n > 0, not (last and n == 3))
                    for j in range(2):
                        binary(m, 2 * n + j)

            every_quad(dve, first_rows)

            def start_of_layer(k):
                unpack(k, Group(0, 0), 0)
                dve.wait_ge(wh_ready[k], GROUPS)
                nc.vector.tensor_reduce(smax[:, :], s[:, 1, :], AX.X, ALU.max).then_inc(smax_ready, 1)
                if k == 2:
                    edge(nc.vector.tensor_reduce(t1[:, :], wh[:, :, :], AX.X, ALU.add))
                    edge(nc.vector.tensor_scalar(valid[:, :], t1[:, :], 0.0, None, ALU.not_equal))
                    edge(nc.vector.tensor_copy(validb[:, :], valid[:, :]))
                    nc.vector.tensor_scalar(sbig[:, :], s[:, 1, :], BIG, None, ALU.mult)
                    edge(nc.vector.tensor_copy(s1_of_2[:, :], s[:, 0, :]))
                if k != 2:
                    edge(nc.vector.tensor_reduce(h_total[:, :], h_sum[:, :], AX.X, ALU.add))
                    nc.vector.tensor_scalar(h_mean[:, :], ones[:, :], h_total[:, 0:1], 1.0 / N, ALU.mult, ALU.mult)\
                        .then_inc(h_mean_ready, 1)
                dve.wait_ge(S_ready, k + 1 if k < 3 else 6)
                first = nc.vector.tensor_scalar(shift[:, 0:1], S[:, :], ALPHA - 1.0, None, ALU.mult)
                if k == 0:
                    first.then_inc(acc_free[0], 1)
                nc.vector.tensor_scalar(shift[:, 1:2], S[:, :], -ALPHA, None, ALU.mult)
                nc.vector.tensor_scalar(t2[:, :], s[:, 0, :], S[:, 0:1], 0.0, ALU.add, ALU.max)\
                    .then_inc(shift_ready, 1)
                dve.wait_ge(exps_ready, k + 1)
                if k == 2:
                    edge(nc.vector.scalar_tensor_tensor(D[:, :], D[:, :], LIFT, valid[:, :], ALU.mult, ALU.mult))
                else:
                    edge(nc.vector.tensor_scalar(D[:, :], D[:, :], LIFT, None, ALU.mult))
                nc.vector.tensor_copy(vals[:, :, F], D[:, :])

            def values(c):
                t = slice(c * JC, (c + 1) * JC)
                nc.vector.tensor_tensor(vals[:, t, 0:F], wh[:, t, :],
                                        D[:, t].rearrange("p (t o) -> p t o", o=1).broadcast_to([P, JC, F]),
                                        ALU.mult).then_inc(vals_ready, 1)

            def make_mean(k):
                dve.wait_ge(mean_done, mean_index[k] + 1)
                edge(nc.vector.tensor_copy(mean[:, :], ps_s[:, 0:F]))

            def thresholds():
                nc.vector.tensor_reduce(least[:, 0:1], sbig[:, :], AX.X, ALU.min)
                for n in range(GROUPS):
                    last = nc.vector.memset(number[:, n * BLOCKS:(n + 1) * BLOCKS], float(n + 1))
                edge(last)
                nc.vector.tensor_scalar(smax[:, :], least[:, 0:1], -1.0 / BIG, None, ALU.mult).then_inc(smax_ready, 1)
                edge(nc.vector.tensor_scalar(t1[:, :], den[:, :], THR / MASK_VALUE / LIFT * 2.0 ** LN_SHIFT,
                                             2.0 ** -60, ALU.mult, ALU.max))
                nc.vector.tensor_scalar(t2[:, :], s1_of_2[:, :], S[:, 0:1], None, ALU.add).then_inc(log_arg, 1)
                dve.wait_ge(log_ready, 1)
                edge(nc.vector.scalar_tensor_tensor(t2[:, :], t2[:, :], ALPHA, t2[:, :], ALU.mult, ALU.max))
                edge(nc.vector.scalar_tensor_tensor(t1[:, :], t1[:, :], -LN_SHIFT * float(np.log(2.0)), t2[:, :],
                                                    ALU.add, ALU.add))
                edge(nc.vector.scalar_tensor_tensor(t1[:, :], t1[:, :], 1.0 / ALPHA, t1[:, :], ALU.mult, ALU.min))
                edge(nc.vector.tensor_tensor(tau[:, :], t1[:, :], s1_of_2[:, :], ALU.subtract))
                dve.wait_ge(S_ready, 4)
                edge(nc.vector.tensor_scalar(least[:, 1:2], found[:, 0:1], -1.0, None, ALU.mult))
                edge(nc.vector.scalar_tensor_tensor(t1[:, :], tau[:, :], least[:, 1:2], number[:, :],
                                                    ALU.is_ge, ALU.mult))
                nc.vector.tensor_reduce(smax[:, :], t1[:, :], AX.X, ALU.max).then_inc(smax_ready, 1)
                dve.wait_ge(S_ready, 5)
                nc.vector.tensor_scalar(redo_groups[:, :], found[:, 1:2], 1.0, None, ALU.max)\
                    .then_inc(redo_known, 1)
                dve.wait_ge(redo_known, 1)

            def column(t, i):
                return t[:, i:i + 1]

            def unpack(sw, g, c):
                kind = SWEEPS[sw][1]
                done = (g.value + groups_before[sw]) * KT + c * JC
                buf = 0 if sw == 0 else c % 2
                if sw == 0:
                    if not isinstance(done, int) or done > 0:
                        dve.wait_ge(q_ready[0], done)
                    dve.wait_ge(bits_ready, g.value * CHUNKS + (c + 1))
                if kind == "counted":
                    if not isinstance(done, int) or done >= 2 * JC:
                        dve.wait_ge(q_used[own[sw]], done - JC)
                for b in range(16):
                    op, amount = (ALU.logical_shift_left, 14 - b) if b <= 14 else (ALU.logical_shift_right, 1)
                    last = nc.vector.tensor_scalar(
                        mask[:, buf, :, b * WORDS:(b + 1) * WORDS],
                        bits[:, g.value, c * JC:(c + 1) * JC, :], amount, ONE, op, ALU.bitwise_and)
                last.then_inc(mask_ready[own[sw]], 1)

            def chunk(sw, g, c, middle):
                kind = SWEEPS[sw][1]
                done = (g.value + groups_before[sw]) * KT + c * JC
                buf = 0 if sw == 0 else c % 2
                dve.wait_ge(mask_ready[own[sw]], (g.value + groups_before[sw]) * CHUNKS + (c + 1))
                for j in range(JC):
                    if kind == "kept" and j % 2 == 0:
                        t = g.value * (KT // 2) + (c * JC + j) // 2
                        dve.wait_ge(keep_ready, t + 1)
                        pair = mask_bf[:, buf, j:j + 2, :]
                        nc.vector.tensor_tensor(pair, pair, keep[:, ((c * JC + j) // 2) % VRING, :, :], ALU.min)\
                            .then_inc(mask_kept, 1)
                        dve.wait_ge(mask_kept, t + 1)
                    tile = done + j
                    if (c * JC + j >= RING if sw == REDO else not isinstance(tile, int) or tile >= RING):
                        dve.wait_ge(q_used[own[sw]], tile + (1 - RING))
                    nc.vector.scalar_tensor_tensor(
                        q[:, j % RING, :], rrow[:, g.parity, :], column(R, c * JC + j), mask_bf[:, buf, j, :],
                        ALU.max, ALU.mult).then_inc(q_ready[own[sw]], 1)
                    if j == JC // 2 - 1:
                        middle()

            OUT_STEPS = {"full": 4, "counted": 5, "kept": 1}

            def scales_of_outputs(sw, g):
                k, kind = SWEEPS[sw]
                if kind == "kept":
                    return
                a = acc[g.parity]
                chain = Chain(dve, out_chain[sw])
                chain.at(g.value * OUT_STEPS[kind])
                dve.wait_ge(q_used[own[sw]], (g.value + (groups_before[sw] + 1)) * KT)
                dens = a[:, :, F:2 * (F + 1):F + 1]
                chain(nc.vector.tensor_copy(den4[:, :].rearrange("p (a b) -> p a b", a=2), dens))
                chain(nc.vector.tensor_scalar(none4[:, :], den4[:, :], 0.0, None, ALU.is_equal))
                chain(nc.vector.tensor_tensor(den4[:, :], den4[:, :], none4[:, :], ALU.add))
                last = nc.vector.reciprocal(rec4[:, :], den4[:, :])
                if kind == "counted":
                    chain(last)
                    cols = bass.ds(g.value * BLOCKS, BLOCKS)
                    counts = a[:, 0, 2 * (F + 1):2 * (F + 1) + BLOCKS]
                    nc.vector.tensor_tensor(den[:, cols], den4[:, :], none4[:, :], ALU.subtract)
                    last = nc.vector.scalar_tensor_tensor(kappa[:, cols], counts, 1.0 / MASK_VALUE, rec4[:, :],
                                                          ALU.mult, ALU.mult)
                last.then_inc(rec_ready[sw], 1)

            def outputs(sw, g):
                k, kind = SWEEPS[sw]
                chain = Chain(dve, out_chain[sw])
                chain.at((g.value + 1) * OUT_STEPS[kind] - 1)
                dve.wait_ge(acc_free[own[sw]], g.value + (groups_before[sw] + (1 if sw == REDO else 2)))
                if kind == "full":
                    for b in range(BLOCKS):
                        last = nc.vector.scalar_tensor_tensor(o[:, b, :], mean[:, :], none4[:, b:b + 1], o[:, b, :],
                                                              ALU.mult, ALU.add)
                else:
                    own_rows = wh[:, bass.ds(g.value * BLOCKS, BLOCKS), :]
                    if sw == REDO:
                        dve.wait_ge(wh_rows_in, g.value * 16 + 16)
                        own_rows = wh_rows[:, :, :]
                    last = nc.vector.tensor_tensor(o[:, :, :], o[:, :, :], own_rows, ALU.add)
                if k == 0:
                    chain(last)
                else:
                    last.then_inc(elu_arg[sw], 1)

            def new_rows(sw, g):
                k, kind = SWEEPS[sw]
                xn = xnew[:, :, :]
                dve.wait_ge(x_in[sw][g.parity], g.half * 16 + 16)
                if k == 0:
                    nc.vector.tensor_tensor(xn, xin[:, :, :], o[:, :, :], ALU.add).then_inc(x_new[sw], 1)
                else:
                    chain = Chain(dve, out_chain[sw])
                    chain.at((g.value + 1) * OUT_STEPS[kind] - 1)
                    dve.wait_ge(elu_exp[sw], g.value + 1)
                    chain(nc.vector.scalar_tensor_tensor(o[:, :, :], o[:, :, :], 0.0, xin[:, :, :],
                                                         ALU.max, ALU.add))
                    nc.vector.scalar_tensor_tensor(xn, e[:, :, :], -1.0, o[:, :, :], ALU.add, ALU.add)\
                        .then_inc(x_new[sw], 1)
                dve.wait_ge(x_new[sw], g.value + 1)
                if k < 3:
                    stats_of(next_projection(sw), xn, g)

            def rows_scaled(sw, g):
                k, kind = SWEEPS[sw]
                if k < 3:
                    scales_of(next_projection(sw), g)

            def body(sw):
                def group(g, before, more):
                    n = rows_of[sw] * g.value + (groups_before[sw] + rows_of[sw])
                    dve.wait_ge(row_ready[own[sw]], n)
                    for c in range(CHUNKS):
                        def middle():
                            if before and c == 1:
                                outputs(sw, before)
                            if before and c == 2:
                                new_rows(sw, before)
                        first = before is None and sw != REDO
                        if first:
                            values(c)
                        if not (first and c == 0):
                            unpack(sw, g, c)
                        chunk(sw, g, c, middle)
                        if first and c == 0 and sw != 2:
                            make_mean(sw)
                        if before and c == 0:
                            scales_of_outputs(sw, before)
                        if before and c == 2:
                            rows_scaled(sw, before)
                return group

            def last_tail(sw):
                def tail(g):
                    scales_of_outputs(sw, g)
                    outputs(sw, g)
                    new_rows(sw, g)
                    rows_scaled(sw, g)
                return tail

            for sw in MAIN:
                start_of_layer(sw)
                every_group(dve, body(sw), last_tail(sw))
                if sw == 2:
                    thresholds()
                    with dve.Fori(0, dve.value_load(redo_groups[0:1, 0:1], min_val=1, max_val=GROUPS)) as p:
                        g = RedoGroup(p)
                        body(REDO)(g, None, False)
                        last_tail(REDO)(g)
                        dve.wait_ge(wh_ready[REPROJECT], g.value + 1)

        @block.tensor
        def _(pe):
            def transposes(k, g):
                pe.wait_ge(h_ready[k], g.value + 1)
                for b in range(BLOCKS):
                    last = nc.tensor.transpose(ps_tr[:, b * P:(b + 1) * P], h[:, b, :], ident[:, :])
                last.then_inc(tr_done[k], 1)

            def project(k, g):
                pe.wait_ge(hT_ready[k], g.value + 1)
                for b in range(BLOCKS):
                    last = nc.tensor.matmul(projected[:, b // 2, b % 2, :], hT[:, b, :], w_sb[:, layer_of(k), :],
                                            start=True, stop=True)
                last.then_inc(wh_done[k], 1)

            pe.wait_ge(weights_in, 16 * 12)
            pe.wait_ge(consts_ready, CONSTS)
            for k in range(4):
                last = nc.tensor.transpose(ps_tr[:, k * P:(k + 1) * P], w_sb[:, k, 0:F], ident[:, :])
            last.then_inc(wT_done, 1)
            pe.wait_ge(wT_copied, 1)
            for k in range(4):
                last = nc.tensor.matmul(ps_s[:, 2 * k:2 * k + 2], wT[:, k, :], a_sb[:, k, :], start=True, stop=True)
            last.then_inc(wa_done, 1)
            pe.wait_ge(wa_copied, 1)

            def pack(pieces_before, chunks_before, i, slot):
                if i == 0 and (not isinstance(chunks_before, int) or chunks_before > 0):
                    pe.wait_ge(bits_ready, chunks_before)
                pe.wait_ge(adj_binary, pieces_before + 1)
                for t in range(AJ):
                    at = (i * AJ + t) * WORDS
                    for b in range(BLOCKS):
                        last = nc.tensor.matmul(ps_pack[:, at:at + WORDS], adj_bf[:, slot, b, t * P:(t + 1) * P],
                                                packer[:, b, :], start=(b == 0), stop=(b == BLOCKS - 1))
                last.then_inc(adj_packed, 1)

            def first_rows(m, last):
                for n in range(4):
                    g = Group(m * 2 + n // 2, n % 2)
                    transposes(0, g)
                    for j in range(2):
                        pack(m * QP + (2 * n + j), m, 2 * n + j, j)
                    project(0, g)

            every_quad(pe, first_rows)

            def spread(sw, g, n):
                if n < rows_of[sw]:
                    done = rows_of[sw] * g.value + (groups_before[sw] + n)
                    pe.wait_ge(diag_ready[own[sw]], done + 1)
                    if (n == 1 if sw == REDO else not isinstance(done, int) or done > 0):
                        pe.wait_ge(row_ready[own[sw]], done)
                    for b in range(BLOCKS):
                        last = nc.tensor.matmul(ps_bc[:, b * P:(b + 1) * P], ones[:, :], diag[:, b, :],
                                                start=True, stop=True)
                    last.then_inc(row_done[own[sw]], 1)

            def mean_row(k):
                pe.wait_ge(h_mean_ready, mean_index[k] + 1)
                nc.tensor.matmul(ps_s[:, 0:F], h_mean[:, :], w_sb[:, k, 0:F], start=True, stop=True)\
                    .then_inc(mean_done, 1)

            def sweep_chunk(sw, g, c, middle, more):
                kind = SWEEPS[sw][1]
                a = acc[g.parity]
                for j in range(JC):
                    t = c * JC + j
                    pe.wait_ge(q_ready[own[sw]], (g.value + groups_before[sw]) * KT + (t + 1))
                    for b in range(BLOCKS):
                        at = (b % 2) * (F + 1)
                        last = nc.tensor.matmul(a[:, b // 2, at:at + F + 1], q[:, j % RING, b * P:(b + 1) * P],
                                                vals[:, t, :], start=(t == 0 and b % 2 == 0), stop=(t == KT - 1),
                                                skip_group_check=True)
                    if kind == "counted":
                        for b in range(BLOCKS):
                            at = 2 * (F + 1) + b
                            last = nc.tensor.matmul(a[:, 0, at:at + 1], mask_bf[:, c % 2, j, b * P:(b + 1) * P],
                                                    validb[:, t:t + 1], start=False, stop=(t == KT - 1),
                                                    skip_group_check=True)
                    last.then_inc(q_used[own[sw]], 1)
                    if sw == 0 and more and j % AJ == AJ - 1:
                        to = after(g)
                        pack(to.value * PIECES + t // AJ, to.value * CHUNKS + c, j // AJ, (j // AJ) % BIN_RING)
                    if j == JC // 2 - 1:
                        middle()

            def body(sw):
                k, kind = SWEEPS[sw]
                projects = k < 3

                def group(g, before, more):
                    if sw != REDO and (not isinstance(g.value, int) or g.value + groups_before[sw] > 0):
                        pe.wait_ge(acc_free[own[sw]], g.value + groups_before[sw])
                    for c in range(CHUNKS):
                        def middle():
                            if c == 3 and more:
                                spread(sw, after(g), 1)
                            if c == 3 and before and projects:
                                transposes(k + 1, before)
                        if before is None and sw != REDO:
                            pe.wait_ge(vals_ready, CHUNKS * sw + c + 1)
                        sweep_chunk(sw, g, c, middle, more)
                        if c == 1 and more:
                            spread(sw, after(g), 0)
                        if c == 3 and before and projects:
                            project(k + 1, before)
                return group

            def last_tail(sw):
                def tail(g):
                    if SWEEPS[sw][0] < 3:
                        transposes(next_projection(sw), g)
                        project(next_projection(sw), g)
                return tail

            for sw in MAIN:
                if sw != 2:
                    mean_row(sw)
                spread(sw, Group(0, 0), 0)
                every_group(pe, body(sw), last_tail(sw))
                if sw == 2:
                    pe.wait_ge(redo_known, 1)
                    with pe.Fori(0, pe.value_load(redo_groups[0:1, 0:1], min_val=1, max_val=GROUPS)) as p:
                        g = RedoGroup(p)
                        spread(REDO, g, 0)
                        spread(REDO, g, 1)
                        body(REDO)(g, None, False)
                        last_tail(REDO)(g)
                        pe.wait_ge(wh_ready[REPROJECT], g.value + 1)

        @block.scalar
        def _(act):
            act.wait_ge(wT_done, 1)
            nc.scalar.activation(wT[:, :, :], ps_tr[:, :].rearrange("p (k f) -> p k f", k=4), ACT.Copy)\
                .then_inc(wT_copied, 1)
            act.wait_ge(wa_done, 1)
            nc.scalar.activation(w_sb[:, :, F:F + 2], ps_s[:, 0:8].rearrange("p (k c) -> p k c", k=4), ACT.Copy)\
                .then_inc(wa_copied, 1)

            def deviations(k, g):
                act.wait_ge(var_ready[k], g.value + 1)
                nc.scalar.activation(sd[:, :], ve[:, :], ACT.Sqrt).then_inc(sd_ready[k], 1)

            def normalised(k, xt, g):
                act.wait_ge(norm_ready[k], g.value + 1)
                for b in range(BLOCKS):
                    last = nc.scalar.activation(h[:, b, :], xt[:, b, :], ACT.Relu, bias=nm[:, b:b + 1],
                                                scale=rs[:, b:b + 1])
                last.then_inc(h_ready[k], 1)

            def copy_hT(k, g):
                act.wait_ge(tr_done[k], g.value + 1)
                nc.scalar.activation(hT[:, :, :], ps_tr[:, :].rearrange("p (b f) -> p b f", b=BLOCKS), ACT.Copy,
                                     accum_out=h_sum[:, bass.ds(g.value, 1)]).then_inc(hT_ready[k], 1)

            def copy_wh(k, g):
                act.wait_ge(wh_done[k], g.value + 1)
                cols = bass.ds(g.value * BLOCKS, BLOCKS)
                nc.scalar.activation(wh[:, cols, :].rearrange("p (a b) f -> p a b f", a=2),
                                     projected[:, :, :, 0:F], ACT.Copy)
                nc.scalar.activation(s[:, :, cols].rearrange("p c (a b) -> p a b c", a=2),
                                     projected[:, :, :, F:F + 2], ACT.Copy).then_inc(wh_ready[k], 1)

            act.wait_ge(consts_ready, CONSTS)

            def binary(pieces_before, rounds, slot, to):
                act.wait_ge(adj_in[slot], rounds * 16 + 16)
                act.wait_ge(adj_packed, pieces_before + (1 - BIN_RING))
                nc.scalar.activation(adj_bf[:, to, :, :], adj_int[:, slot, :, :], ACT.Sigmoid, scale=STEEP,
                                     bias=threshold[:, 0:1]).then_inc(adj_binary, 1)

            def words(g, c):
                act.wait_ge(adj_packed, (g * CHUNKS + c + 1) * QP)
                nc.scalar.activation(bits[:, g, bass.ds(c * JC, JC), :],
                                     ps_pack[:, :].rearrange("p (t n) -> p t n", t=JC), ACT.Copy)\
                    .then_inc(bits_ready, 1)

            deviations(0, Group(0, 0))

            def first_rows(m, last):
                for n in range(4):
                    g = Group(m * 2 + n // 2, n % 2)
                    normalised(0, [xin, xnew][g.parity][:, :, :], g)
                    copy_hT(0, g)
                    if not (last and n == 3):
                        deviations(0, after(g))
                    if n == 3:
                        words(0, m)
                    copy_wh(0, g)

            every_quad(act, first_rows)

            def diagonal(sw, g, n):
                col = [r, tau][n]
                for b in range(BLOCKS):
                    last = nc.scalar.activation(diag[:, b, :], ident[:, :], ACT.Copy,
                                                scale=col[:, bass.ds(g.value * BLOCKS + b, 1)])
                last.then_inc(diag_ready[own[sw]], 1)

            def copy_rows(sw, g, n):
                if n < rows_of[sw]:
                    row = [rrow[:, g.parity, :], taurow[:, :]][n]
                    act.wait_ge(row_done[own[sw]], rows_of[sw] * g.value + (groups_before[sw] + n + 1))
                    nc.scalar.activation(row, ps_bc[:, :], ACT.Copy).then_inc(row_ready[own[sw]], 1)

            def scaled_sums(sw, g):
                kind = SWEEPS[sw][1]
                act.wait_ge(x_in[sw][g.parity], g.half * 16 + 16)
                if kind == "kept":
                    act.wait_ge(q_used[1], g.value * KT + KT)
                else:
                    act.wait_ge(rec_ready[sw], g.value + 1)
                for b in range(BLOCKS):
                    at = (b % 2) * (F + 1)
                    scale = rec4[:, b:b + 1] if kind == "full" else kappa[:, bass.ds(g.value * BLOCKS + b, 1)]
                    last = nc.scalar.activation(o[:, b, :], acc[g.parity][:, b // 2, at:at + F], ACT.Copy,
                                                scale=scale)
                last.then_inc(acc_free[own[sw]], 1)

            def elu_exp_of(sw, g):
                act.wait_ge(elu_arg[sw], g.value + 1)
                nc.scalar.activation(e[:, :, :], o[:, :, :], ACT.Relu, scale=-1.0).then_inc(elu_neg[sw], 1)
                act.wait_ge(elu_neg[sw], g.value + 1)
                nc.scalar.activation(e[:, :, :], e[:, :, :], ACT.Exp, scale=-1.0).then_inc(elu_exp[sw], 1)

            def keep_tile(g, t):
                n = g.value * (KT // 2) + t
                if t >= VRING:
                    act.wait_ge(mask_kept, n + (1 - VRING))
                for j in range(2):
                    last = nc.scalar.activation(keep[:, t % VRING, j, :], taurow[:, :], ACT.Relu,
                                                scale=-BIG, bias=sbig[:, 2 * t + j:2 * t + j + 1])
                last.then_inc(keep_ready, 1)

            def body(sw):
                def group(g, before, more):
                    due = []
                    if before:
                        due.append((QP + 1, lambda: scaled_sums(sw, before)))
                    if more:
                        due.append((QP + 2, lambda: diagonal(sw, after(g), 0)))
                    if before and sw > 0:
                        due.append((QP + 5, lambda: elu_exp_of(sw, before)))
                    if more:
                        due.append((2 * QP, lambda: copy_rows(sw, after(g), 0)))
                    if before and sw < 3:
                        due.append((2 * QP + 5, lambda: deviations(sw + 1, before)))
                        due.append((3 * QP + 2, lambda: normalised(sw + 1, xnew[:, :, :], before)))
                        due.append((3 * QP + 5, lambda: copy_hT(sw + 1, before)))
                        due.append((PIECES + 1, lambda: copy_wh(sw + 1, before)))
                    if sw == 0 and more:
                        to = after(g).value
                        for i in range(PIECES + 1):
                            while due and due[0][0] <= i:
                                due.pop(0)[1]()
                            if i % QP == 1 and i > 1:
                                words(to, i // QP - 1)
                            if i < PIECES:
                                binary(to * PIECES + i, to * (PIECES // ADJ_RING) + i // ADJ_RING, i % ADJ_RING,
                                       i % BIN_RING)
                        words(to, CHUNKS - 1)
                    for _, do in due:
                        do()
                return group

            def last_tail(sw):
                k, kind = SWEEPS[sw]

                def tail(g):
                    scaled_sums(sw, g)
                    if k > 0:
                        elu_exp_of(sw, g)
                    if k < 3:
                        to = next_projection(sw)
                        deviations(to, g)
                        normalised(to, xnew[:, :, :], g)
                        copy_hT(to, g)
                        copy_wh(to, g)
                return tail

            for sw in MAIN:
                act.wait_ge(shift_ready, sw + 1)
                nc.scalar.activation(R[:, :], s[:, 1, :], ACT.Exp, scale=1.0 - ALPHA, bias=shift[:, 0:1])
                nc.scalar.activation(D[:, :], s[:, 1, :], ACT.Exp, scale=ALPHA, bias=shift[:, 1:2])
                nc.scalar.activation(r[:, :], t2[:, :], ACT.Exp, scale=ALPHA - 1.0).then_inc(exps_ready, 1)
                act.wait_ge(exps_ready, sw + 1)
                diagonal(sw, Group(0, 0), 0)
                copy_rows(sw, Group(0, 0), 0)
                if sw == 2:
                    act.wait_ge(redo_stored, 16)
                every_group(act, body(sw), last_tail(sw))
                if sw == 2:
                    act.wait_ge(log_arg, 1)
                    nc.scalar.activation(t1[:, :], t1[:, :], ACT.Ln).then_inc(log_ready, 1)
                    act.wait_ge(redo_known, 1)
                    with act.Fori(0, act.value_load(redo_groups[0:1, 0:1], min_val=1, max_val=GROUPS)) as p:
                        g = RedoGroup(p)
                        for n in range(2):
                            diagonal(REDO, g, n)
                            copy_rows(REDO, g, n)
                        act.wait_ge(row_ready[1], g.value * 2 + 2)
                        for t in range(KT // 2):
                            keep_tile(g, t)
                        last_tail(REDO)(g)


_WS = [f"L{k}_gnn_W" for k in range(4)]
_AS = [f"L{k}_gnn_a" for k in range(4)]


def kernel(**inputs):
    import numpy as _np
    import concourse.bacc as _bacc
    from concourse import mybir as _mybir
    from concourse.bass_utils import run_bass_kernel_spmd as _run

    nc = _bacc.Bacc("TRN2", target_bir_lowering=False, num_devices=1)
    arrays, aps = {}, {}
    for name in ["x", "adj"] + _WS + _AS:
        a = _np.ascontiguousarray(inputs[name])
        arrays[f"in_{name}_dram"] = a
        aps[name] = nc.dram_tensor(f"in_{name}_dram", a.shape, _mybir.dt.from_np(a.dtype), kind="ExternalInput").ap()
    out = nc.dram_tensor("out_0_dram", (N, F), F32, kind="ExternalOutput").ap()
    build(nc, aps["x"], aps["adj"], [aps[n] for n in _WS], [aps[n] for n in _AS], out)
    r = _run(nc, [arrays], core_ids=[0])
    return r.results[0]["out_0_dram"]
```
